# Optimizing a Trainium2 kernel written in Bass

```python
import numpy as np
import jax
import jax.numpy as jnp

def _softmax(x, axis=-1):
    return jax.nn.softmax(x, axis=axis)

def _gelu(x):
    return jax.nn.gelu(x, approximate=True)

def _silu(x):
    return jax.nn.silu(x)

def _sigmoid(x):
    return jax.nn.sigmoid(x)

def _layernorm(x, axis=-1, eps=1e-05):
    m = jnp.mean(x, axis=axis, keepdims=True)
    v = jnp.var(x, axis=axis, keepdims=True)
    return (x - m) / jnp.sqrt(v + eps)

def _scatter_add(tgt, idx, src, axis=0):
    return tgt.at[idx].add(src)

def _segment_sum(src, seg, n):
    return jax.ops.segment_sum(src, seg, n)
kernel_name = 'mk_decoder_postln_d1_seqx_r8_3126d4'

def setup_inputs(seed: int=0):
    np.random.seed(seed)
    _w = jnp.asarray

    def _rec_inputs():
        import jax
        import jax.numpy as jnp
        _rk = jax.random.key(seed)
        x = -0.000125 + 0.9999 * jax.random.normal(jax.random.fold_in(_rk, 1), (2, 256, 512), jnp.float32)
        _lenS = 256 - jax.random.randint(jax.random.fold_in(_rk, 7), (2,), 0, max(1, 256 // 4) + 1, jnp.int32)
        _lenS2 = 512 - jax.random.randint(jax.random.fold_in(_rk, 8), (2,), 0, max(1, 512 // 4) + 1, jnp.int32)
        _ctx_4096P = jax.random.normal(jax.random.fold_in(_rk, 11), (2, 16, 512), jnp.float32)
        _ctx_4096c = jax.random.dirichlet(jax.random.fold_in(_rk, 511), 0.3 * jnp.ones((16,), jnp.float32), (2, 512))
        _ctx_4096t = jnp.einsum('bsk,bkd->bsd', _ctx_4096c, _ctx_4096P)
        _ctx_4096t = _ctx_4096t * jax.lax.rsqrt(jnp.mean(jnp.square(_ctx_4096t)) + 1e-12) * 0.953939
        ctx_4096 = -5.72187e-05 + 0.999849 * (_ctx_4096t + 0.3 * jax.random.normal(jax.random.fold_in(_rk, 611), (2, 512, 512), jnp.float32))
        return (x, ctx_4096)
    x, ctx_4096 = _rec_inputs()

    def _L0_attn_setup():
        import jax, jax.numpy as jnp
        import numpy as np
        import math
        D_MODEL = 512
        N_HEADS = 32
        HEAD_DIM = D_MODEL // N_HEADS
        CLIP_QKV = 8.0
        ALIBI_BIAS_MAX = 8
        LN_EPS = 1e-05

        def _alibi_slopes(total_num_heads: int, alibi_bias_max: int) -> jnp.ndarray:
            next_p2 = 2 ** math.ceil(math.log2(total_num_heads))
            m = jnp.arange(1, next_p2 + 1, dtype=jnp.float32) * (alibi_bias_max / next_p2)
            slopes = 1.0 / jnp.power(2.0, m)
            if next_p2 != total_num_heads:
                slopes = jnp.concatenate([slopes[1::2], slopes[::2]])[:total_num_heads]
            return slopes

        def _layer_norm(x, w, b):
            mu = jnp.mean(x, axis=-1, keepdims=True)
            var = jnp.var(x, axis=-1, keepdims=True)
            return (x - mu) * jax.lax.rsqrt(var + LN_EPS) * w + b
        key = jax.random.key(seed)
        k0, k1, k2 = jax.random.split(key, 3)
        B, S = (2, 256)
        return {'hidden_states': jax.random.normal(k0, (B, S, D_MODEL), dtype=jnp.float32), 'w_qkv': jax.random.normal(k1, (3 * D_MODEL, D_MODEL), dtype=jnp.float32) * 0.02, 'q_ln_w': jnp.ones((D_MODEL,), jnp.float32), 'q_ln_b': jnp.zeros((D_MODEL,), jnp.float32), 'k_ln_w': jnp.ones((D_MODEL,), jnp.float32), 'k_ln_b': jnp.zeros((D_MODEL,), jnp.float32), 'w_out': jax.random.normal(k2, (D_MODEL, D_MODEL), dtype=jnp.float32) * 0.02}
    _L0_attn_all = _L0_attn_setup()
    _L0_attn_in = {k: v for k, v in _L0_attn_all.items() if k in ('w_qkv', 'q_ln_w', 'q_ln_b', 'k_ln_w', 'k_ln_b', 'w_out')}
    del _L0_attn_all

    def _L0_xattn_setup():
        import jax, jax.numpy as jnp
        import numpy as np
        QMIN = 0.0
        QMAX = 255.0

        def fake_quant(x, scale, zp):
            s = scale.reshape(())
            z = zp.reshape(())
            q = jnp.clip(jnp.round(x / s + z), QMIN, QMAX)
            return (q - z) * s
        key = jax.random.key(seed)
        k1, k2 = jax.random.split(key)
        B, M, K, N = (4, 256, 512, 512)
        x1 = jax.random.normal(k1, (B, M, K), dtype=jnp.float32)
        x2 = jax.random.normal(k2, (B, K, N), dtype=jnp.float32)
        x1_scale = jnp.full((1,), 8.0 / 255.0, dtype=jnp.float32)
        x1_zp = jnp.full((1,), 128.0, dtype=jnp.float32)
        x2_scale = jnp.full((1,), 8.0 / 255.0, dtype=jnp.float32)
        x2_zp = jnp.full((1,), 128.0, dtype=jnp.float32)
        return {'x1': x1, 'x2': x2, 'x1_scale': x1_scale, 'x1_zp': x1_zp, 'x2_scale': x2_scale, 'x2_zp': x2_zp}
    _L0_xattn_all = _L0_xattn_setup()
    _L0_xattn_in = {k: v for k, v in _L0_xattn_all.items() if k in ('x1_scale', 'x1_zp', 'x2_scale', 'x2_zp')}
    del _L0_xattn_all

    def _L0_ffn_setup():
        import jax, jax.numpy as jnp
        import numpy as np
        NUM_EXPERTS = 8
        TOP_K = 2
        RANK = 16
        LORA_ALPHA = 32
        SCALING = LORA_ALPHA / RANK
        key = jax.random.key(seed)
        ks = jax.random.split(key, 6)
        B, S, D_IN, D_OUT = (4, 256, 512, 512)
        x = jax.random.normal(ks[0], (B, S, D_IN), dtype=jnp.float32)
        W_base = jax.random.normal(ks[1], (D_OUT, D_IN), dtype=jnp.float32) * 0.02
        b_base = jax.random.normal(ks[2], (D_OUT,), dtype=jnp.float32) * 0.02
        W_router = jax.random.normal(ks[3], (NUM_EXPERTS, D_IN), dtype=jnp.float32) * 0.02
        A = jax.random.normal(ks[4], (NUM_EXPERTS, RANK, D_IN), dtype=jnp.float32) * 0.02
        Bm = jax.random.normal(ks[5], (D_OUT, RANK), dtype=jnp.float32) * 0.02
        Bm = jnp.broadcast_to(Bm, (NUM_EXPERTS, D_OUT, RANK)) * jnp.arange(1, NUM_EXPERTS + 1, dtype=jnp.float32)[:, None, None] * 0.2
        return {'x': x, 'W_base': W_base, 'b_base': b_base, 'W_router': W_router, 'A': A, 'B': Bm}
    _L0_ffn_all = _L0_ffn_setup()
    _L0_ffn_in = {k: v for k, v in _L0_ffn_all.items() if k in ('W_base', 'b_base', 'W_router', 'A', 'B')}
    del _L0_ffn_all
    return {'x': x, 'ctx_4096': ctx_4096, 'L0_attn_w_qkv': _L0_attn_in['w_qkv'], 'L0_attn_q_ln_w': _L0_attn_in['q_ln_w'], 'L0_attn_q_ln_b': _L0_attn_in['q_ln_b'], 'L0_attn_k_ln_w': _L0_attn_in['k_ln_w'], 'L0_attn_k_ln_b': _L0_attn_in['k_ln_b'], 'L0_attn_w_out': _L0_attn_in['w_out'], 'L0_xattn_x1_scale': _L0_xattn_in['x1_scale'], 'L0_xattn_x1_zp': _L0_xattn_in['x1_zp'], 'L0_xattn_x2_scale': _L0_xattn_in['x2_scale'], 'L0_xattn_x2_zp': _L0_xattn_in['x2_zp'], 'L0_ffn_W_base': _L0_ffn_in['W_base'], 'L0_ffn_b_base': _L0_ffn_in['b_base'], 'L0_ffn_W_router': _L0_ffn_in['W_router'], 'L0_ffn_A': _L0_ffn_in['A'], 'L0_ffn_B': _L0_ffn_in['B']}

def reference(x, ctx_4096, L0_attn_w_qkv, L0_attn_q_ln_w, L0_attn_q_ln_b, L0_attn_k_ln_w, L0_attn_k_ln_b, L0_attn_w_out, L0_xattn_x1_scale, L0_xattn_x1_zp, L0_xattn_x2_scale, L0_xattn_x2_zp, L0_ffn_W_base, L0_ffn_b_base, L0_ffn_W_router, L0_ffn_A, L0_ffn_B):
    import jax
    import jax.numpy as jnp

    def _L0_attn_ref(hidden_states, w_qkv, q_ln_w, q_ln_b, k_ln_w, k_ln_b, w_out):
        import jax, jax.numpy as jnp
        import numpy as np
        import math
        D_MODEL = 512
        N_HEADS = 32
        HEAD_DIM = D_MODEL // N_HEADS
        CLIP_QKV = 8.0
        ALIBI_BIAS_MAX = 8
        LN_EPS = 1e-05

        def _alibi_slopes(total_num_heads: int, alibi_bias_max: int) -> jnp.ndarray:
            next_p2 = 2 ** math.ceil(math.log2(total_num_heads))
            m = jnp.arange(1, next_p2 + 1, dtype=jnp.float32) * (alibi_bias_max / next_p2)
            slopes = 1.0 / jnp.power(2.0, m)
            if next_p2 != total_num_heads:
                slopes = jnp.concatenate([slopes[1::2], slopes[::2]])[:total_num_heads]
            return slopes

        def _layer_norm(x, w, b):
            mu = jnp.mean(x, axis=-1, keepdims=True)
            var = jnp.var(x, axis=-1, keepdims=True)
            return (x - mu) * jax.lax.rsqrt(var + LN_EPS) * w + b
        B, S, D = hidden_states.shape
        qkv = jnp.einsum('bsd,ed->bse', hidden_states, w_qkv)
        qkv = jnp.clip(qkv, -CLIP_QKV, CLIP_QKV)
        q, k, v = jnp.split(qkv, 3, axis=-1)
        q = _layer_norm(q, q_ln_w, q_ln_b)
        k = _layer_norm(k, k_ln_w, k_ln_b)
        q = q.reshape(B, S, N_HEADS, HEAD_DIM)
        k = k.reshape(B, S, N_HEADS, HEAD_DIM)
        v = v.reshape(B, S, N_HEADS, HEAD_DIM)
        scale = HEAD_DIM ** (-0.5)
        scores = jnp.einsum('bqhd,bkhd->bhqk', q, k) * scale
        pos = jnp.arange(S)
        rel = pos[None, :] - pos[:, None]
        slopes = _alibi_slopes(N_HEADS, ALIBI_BIAS_MAX)
        bias = slopes[:, None, None] * rel.astype(jnp.float32)
        causal = rel <= 0
        scores = jnp.where(causal[None, None], scores + bias[None], -jnp.inf)
        probs = jax.nn.softmax(scores, axis=-1)
        attn = jnp.einsum('bhqk,bkhd->bqhd', probs, v).reshape(B, S, D)
        return jnp.einsum('bsd,ed->bse', attn, w_out)

    def _L0_xattn_ref(x1, x2, x1_scale, x1_zp, x2_scale, x2_zp):
        import jax, jax.numpy as jnp
        import numpy as np
        QMIN = 0.0
        QMAX = 255.0

        def fake_quant(x, scale, zp):
            s = scale.reshape(())
            z = zp.reshape(())
            q = jnp.clip(jnp.round(x / s + z), QMIN, QMAX)
            return (q - z) * s
        q1 = fake_quant(x1, x1_scale, x1_zp)
        q2 = fake_quant(x2, x2_scale, x2_zp)
        return jnp.matmul(q1, q2)

    def _L0_ffn_ref(x, W_base, b_base, W_router, A, B):
        import jax, jax.numpy as jnp
        import numpy as np
        NUM_EXPERTS = 8
        TOP_K = 2
        RANK = 16
        LORA_ALPHA = 32
        SCALING = LORA_ALPHA / RANK
        bs, seq, d_in = x.shape
        T = bs * seq
        xf = x.reshape(T, d_in)
        base = xf @ W_base.T + b_base
        logits = xf @ W_router.T
        rw, sel = jax.lax.top_k(logits, TOP_K)
        rw = jax.nn.softmax(rw, axis=-1)
        onehot = jax.nn.one_hot(sel, NUM_EXPERTS, dtype=rw.dtype)
        w = jnp.einsum('tk,tke->te', rw, onehot)
        h = jnp.einsum('td,erd->ter', xf, A)
        lora = jnp.einsum('ter,te,eor->to', h, w, B) * SCALING
        return (base + lora).reshape(bs, seq, -1)
    x = _layernorm(x + _L0_attn_ref(x, L0_attn_w_qkv, L0_attn_q_ln_w, L0_attn_q_ln_b, L0_attn_k_ln_w, L0_attn_k_ln_b, L0_attn_w_out), axis=-1)
    x = _layernorm(x + _L0_xattn_ref(x, ctx_4096, L0_xattn_x1_scale, L0_xattn_x1_zp, L0_xattn_x2_scale, L0_xattn_x2_zp), axis=-1)
    x = _layernorm(x + _L0_ffn_ref(x, L0_ffn_W_base, L0_ffn_b_base, L0_ffn_W_router, L0_ffn_A, L0_ffn_B), axis=-1)
    return x

_drawn_inputs = setup_inputs


def setup_inputs(seed=0):
    import zlib

    import numpy as np

    out = dict(_drawn_inputs(seed))
    spreads = {'L0_attn_q_ln_w': (1.0, 0.6),
     'L0_attn_q_ln_b': (0.0, 0.508),
     'L0_attn_k_ln_w': (1.0, 0.6),
     'L0_attn_k_ln_b': (0.0, 0.8)}
    factors = {'L0_ffn_b_base': 3.116}
    for name, (base, spread) in spreads.items():
        noise = np.random.default_rng([zlib.crc32(name.encode()), seed]).standard_normal(out[name].shape)
        drawn = base * np.exp(spread * noise) if base else spread * noise
        out[name] = jnp.asarray(drawn.astype(out[name].dtype))
    for name, factor in factors.items():
        out[name] = (out[name] * factor).astype(out[name].dtype)
    return out
```

```python
import numpy as np
import concourse.bass as bass
from concourse import mybir
from contextlib import ExitStack

P = 128
B, S, D = 2, 256, 512
TILES = B * S // P
QT = S // P
KT = D // P
H = 32
DH = D // H
PARTS = 6
PR = PARTS * DH
AUG = 32
HG = 8
NG = H // HG
VW = 32
E = 8
R = 16
ER = E * R
CTX = 512
CT = CTX // P
CLIP = 8.0
EPS = 1e-5
LORA_SCALE = 2.0
MASKED = -1e30
QMAX = 255.0
CENTRE = 128.0
ROUND = 1.5 * 2.0 ** 23

ORDER = [("A", 0), ("N", 0), ("A", 1), ("B", 0), ("N", 1), ("C", 0), ("A", 2), ("E", 0), ("B", 1), ("N", 2), ("C", 1),
         ("F", 0), ("A", 3), ("O", 0), ("E", 1), ("B", 2), ("N", 3), ("C", 2), ("S", 0), ("G", 0), ("F", 1), ("E", 2),
         ("B", 3), ("C", 3), ("O", 1), ("H", 0), ("G", 1), ("F", 2), ("E", 3), ("I", 0), ("O", 2), ("S", 1), ("H", 1),
         ("G", 2), ("F", 3), ("I", 1), ("O", 3), ("H", 2), ("G", 3), ("I", 2), ("H", 3), ("I", 3)]


def bank_uses(keys, slots):
    return {key: (i % slots, i // slots + 1) for i, key in enumerate(keys)}


def blocks_of(t):
    return [(k, k == t) for k in range(t - t % QT, t + 1)]


def build(nc, xT, xrow, wqkvT, ln, woT, ctx4, scal, wbT, arT, loraB, identf, identb, maskc, kaug, qaug, mcols, iota, out):
    fp32, bf16, u32 = mybir.dt.float32, mybir.dt.bfloat16, mybir.dt.uint32
    ALU = mybir.AluOpType
    ACT = mybir.ActivationFunctionType
    AX = mybir.AxisListType

    ctx = ExitStack()
    with ctx:
        def sb(name, shape, dt=fp32):
            return ctx.enter_context(nc.sbuf_tensor(name, shape, dt))

        def pb(name, shape, dt=fp32):
            return ctx.enter_context(nc.psum_tensor(name, shape, dt))

        def sem(name):
            return ctx.enter_context(nc.semaphore(name))

        xT_s = sb("xT_s", [P, TILES, KT, P])
        x_s = sb("x_s", [P, TILES, D])
        wqkv_s = sb("wqkv_s", [P, 3, KT, D])
        ln_s = sb("ln_s", [P, 5, D])
        wo_s = sb("wo_s", [P, KT, D])
        ctx_s = sb("ctx_s", [P, CT, D])
        q2_s = sb("q2_s", [P, 2, CT, D], bf16)
        wb_s = sb("wb_s", [P, KT, D])
        ar_s = sb("ar_s", [P, KT, E + ER])
        lb_s = sb("lb_s", [ER, D])
        idf = sb("idf", [P, P])
        idb = sb("idb", [P, P], bf16)
        mask_s = sb("mask_s", [P, 2, P], bf16)
        ones_b = sb("ones_b", [P, P], bf16)
        qaug_s = sb("qaug_s", [P, QT, P], bf16)
        iota_s = sb("iota_s", [P, E])
        scal_s = sb("scal_s", [P, 4])
        a12 = sb("a12", [P, 2])
        inv_s = sb("inv_s", [P, 2])
        s12 = sb("s12", [P, 1])
        kaa = sb("kaa", [P, 1])
        halfs = sb("halfs", [P, 2])
        kst = sb("kst", [P, QT, H, P], bf16)
        qst = sb("qst", [P, 2, H, P], bf16)
        vaug = sb("vaug", [P, TILES, H, VW])
        lin = sb("lin", [P, 2, D])
        nrm = sb("nrm", [P, 2, D])
        res = sb("res", [P, 2, D])
        stk = sb("stk", [P, 2, H, PR], bf16)
        st6 = sb("st6", [P, 2, 6])
        mv = sb("mv", [P, 2, 2, 2])
        rs2 = sb("rs2", [P, 2, 2])
        ve2 = sb("ve2", [P, 2])
        mx = sb("mx", [P, H])
        md = sb("md", [P, H])
        mtok = sb("mtok", [P, TILES, NG, AUG], bf16)
        mT = sb("mT", [P, P], bf16)
        PTN = 4
        pt = sb("pt", [P, PTN, HG, P])
        osb = sb("osb", [P, 2, D])
        rsum = sb("rsum", [P, 2, H // 2])
        att = sb("att", [P, D])
        attT = sb("attT", [P, KT, P])
        r1 = r2 = r3 = qd = sb("r1", [P, D])
        x1 = x2 = x3 = x_s
        stl = sb("stl", [P, 3, 6])
        mvl = sb("mvl", [P, 3, 2])
        vel = sb("vel", [P, 3, 1])
        rsl = sb("rsl", [P, 3, 1])
        q1b = sb("q1b", [P, D], bf16)
        junk = sb("junk", [P, D], bf16)
        rsq = sb("rsq", [P, 1])
        arq = sb("arq", [P, 1])
        q1T = sb("q1T", [P, KT, P], bf16)
        colc = sb("colc", [P, 2, D])
        xb = sb("xb", [P, 2, D])
        x2T = sb("x2T", [P, 2, KT, P])
        lg = sb("lg", [P, 2, E + ER])
        top = sb("top", [P, 8])
        idx = sb("idx", [P, 8], u32)
        idxf = sb("idxf", [P, 2])
        dl = sb("dl", [P, 1])
        ex = sb("ex", [P, 1])
        den = sb("den", [P, 1])
        w01 = sb("w01", [P, 2])
        wsel = sb("wsel", [P, 2, E])
        hw = sb("hw", [P, E, R])
        hwT = sb("hwT", [P, P])

        G = [pb(f"G{i}", [P, D]) for i in range(2)]
        T = [pb(f"T{i}", [P, D]) for i in range(2)]
        SC = [pb(f"SC{i}", [P, 2 * D]) for i in range(2)]
        gkeys, tkeys, skeys = [], [], []
        for st, t in ORDER:
            if st == "A":
                gkeys += [("A", t, j) for j in range(3)]
            if st == "B":
                tkeys += [("B", t, j, g) for j in range(2) for g in range(NG)]
            if st == "C":
                skeys += [("C", t, g) for g in range(NG * (1 + t % QT))]
                tkeys += [("M", t)]
            if st == "E":
                tkeys += [("E", t, 0), ("E", t, 1)]
                skeys += [("E", t, g, k) for g in range(NG) for k in range(len(blocks_of(t)))]
            if st == "F":
                tkeys += [("F", t, 0), ("F", t, 1), ("FT", t)]
            if st == "O":
                gkeys += [("O", t)]
            if st == "S":
                gkeys += [("S", t)]
            if st == "G":
                tkeys += [("G", t)]
                gkeys += [("G", t)]
            if st == "H":
                tkeys += [("H", t)]
                gkeys += [("H", t)]
            if st == "I":
                gkeys += [("I", t)]
                tkeys += [("I", t)]
        guse, tuse, suse = bank_uses(gkeys, 2), bank_uses(tkeys, 2), bank_uses(skeys, 2)
        g_full, g_free = [sem(f"g_full{i}") for i in range(2)], [sem(f"g_free{i}") for i in range(2)]
        t_full, t_free = [sem(f"t_full{i}") for i in range(2)], [sem(f"t_free{i}") for i in range(2)]
        s_full, s_free = [sem(f"s_full{i}") for i in range(2)], [sem(f"s_free{i}") for i in range(2)]

        ld_x = [sem(f"ld_x{t}") for t in range(TILES)]
        ld_w = [sem(f"ld_w{j}") for j in range(3)]
        names = ("ln id mask kaug qaug mcols xrow wo ctx scal wb ar lb iota").split()
        ld = {n: sem("ld_" + n) for n in names}

        prod = ("const_ready lin_ready v_ready st_ready mv_ready ve_ready rstd_ready n1_ready n2_ready c1_ready r_ready c2_ready "
                "c3_ready stack_ready vones qaug_ready max_ready m1 m2 m3 m4 mT_ready maug_ready exp_ready pv_done "
                "o_ready rsum_ready att_ready attT_ready r1_ready stl_ready mvl_ready vel_ready rsl_ready x1_ready "
                "qd1 qd2 qd3 q1_ready rowsum_ready arq_ready q1T_ready col_ready t1_ready r2_ready x2_ready "
                "xb_ready x2T_ready lg_ready top_ready idx_ready idxf_ready dl_ready ex_ready den_ready w_ready w0_ready w1_ready "
                "ws0 ws1 wsel_ready hw_ready hwT_ready r3_ready x3_ready out_done inv_ready q2a q2b q2_ready sc1 sc2 "
                "qk_transposed wt_done lbias").split()
        s = {n: sem(n) for n in prod}

        block = ctx.enter_context(nc.Block())

        @block.sync
        def _(sp):
            def load(dst, src, signal):
                sp.dma_start(dst, src).then_inc(signal, 16)

            load(xT_s[:, 0, :, :], xT[0], ld_x[0])
            load(scal_s[:, :], scal, ld["scal"])
            for j in range(3):
                load(wqkv_s[:, j, :, :], wqkvT[j], ld_w[j])
            load(ln_s[:, :, :], ln, ld["ln"])
            load(idf[:, :], identf, ld["id"])
            load(idb[:, :], identb, ld["id"])
            load(mask_s[:, :, :], maskc, ld["mask"])
            load(qaug_s[P - AUG:P, :, :], qaug, ld["qaug"])
            load(xT_s[:, 1, :, :], xT[1], ld_x[1])
            load(kst[P - AUG:P, :, :, :], kaug, ld["kaug"])
            for t in range(TILES):
                load(mtok[:, t, :, :], mcols[t % QT], ld["mcols"])
            for t in range(2, TILES):
                load(xT_s[:, t, :, :], xT[t], ld_x[t])
            load(iota_s[:, :], iota, ld["iota"])
            load(x_s[:, :, :], xrow, ld["xrow"])
            load(wo_s[:, :, :], woT, ld["wo"])
            load(ctx_s[:, :, :], ctx4[0], ld["ctx"])
            load(ar_s[:, :, :], arT, ld["ar"])
            load(wb_s[:, :, :], wbT, ld["wb"])
            load(lb_s[:, :], loraB, ld["lb"])
            sp.wait_ge(s["q2_ready"], CT)
            load(ctx_s[:, :, :], ctx4[1], ld["ctx"])
            for t in range(TILES):
                sp.wait_ge(s["x3_ready"], t + 1)
                sp.dma_start(out[t], x3[:, t, :]).then_inc(s["out_done"], 16)
            sp.wait_ge(s["out_done"], 16 * TILES)

        nblk, grp_of, n, m = {}, [], 0, 0
        exp_tiles = [t for st, t in ORDER if st == "E"]
        for t in exp_tiles:
            for g in range(NG):
                for k in range(len(blocks_of(t))):
                    nblk[t, g, k] = n
                    grp_of.append(m)
                    n += 1
                m += 1

        def scores_done(eng, t):
            for g in range(NG - 2, NG):
                for k in range(len(blocks_of(t))):
                    eng.wait_ge(s_full[suse["E", t, g, k][0]], suse["E", t, g, k][1])

        @block.tensor
        def _(pe):
            def begin(full, free, use):
                slot, n = use
                if n > 1:
                    pe.wait_ge(free[slot], n - 1)
                return slot

            def done(free, use):
                pe.wait_ge(free[use[0]], use[1])

            def project(bank, lhs, rhs, kts, stop=True):
                for kt in range(kts):
                    last = nc.tensor.matmul(bank, lhs[:, kt, :], rhs[:, kt, :], start=kt == 0, stop=stop and kt == kts - 1)
                return last

            def stage_a(t):
                pe.wait_ge(ld_x[t], 16)
                for j in range(3):
                    if t == 0:
                        pe.wait_ge(ld_w[j], 16)
                    i = begin(g_full, g_free, guse["A", t, j])
                    project(G[i][:, :], xT_s[:, t, :, :], wqkv_s[:, j, :, :], KT).then_inc(g_full[i], 1)

            def stage_b(t):
                if t == 0:
                    pe.wait_ge(ld["id"], 32)
                for j in range(2):
                    pe.wait_ge(s["c3_ready"], 2 * t + j + 1)
                    for g in range(NG):
                        i = begin(t_full, t_free, tuse["B", t, j, g])
                        tb = T[i][:, :].bitcast(bf16)
                        for c in range(HG):
                            last = nc.tensor.transpose(tb[0:PR, c * P:(c + 1) * P], stk[:, j, g * HG + c, :], idb[:, :])
                        last.then_inc(t_full[i], 1)

            def stage_c(t):
                qt = t % QT
                per = HG // (1 + qt)
                if t == 0:
                    pe.wait_ge(ld["mask"], 16)
                    pe.wait_ge(ld["kaug"], 16)
                pe.wait_ge(s["qaug_ready"], t + 1)
                for j in range(2):
                    for g in range(NG):
                        done(t_free, tuse["B", t, j, g])
                for u in range(H // per):
                    i = begin(s_full, s_free, suse["C", t, u])
                    for bank in range(2):
                        cols = SC[i][:, bank * D:(bank + 1) * D].rearrange("p (h k) -> p h k", k=P * (1 + qt))
                        hb = per // 2
                        nc.tensor.matmul(cols[:, :, qt * P:(qt + 1) * P], idb[:, :],
                                         mask_s[:, 0:1, :].broadcast_to([P, hb, P]), start=True, stop=False,
                                         skip_group_check=True)
                        for c in range(hb):
                            h = u * per + bank * hb + c
                            last = nc.tensor.matmul(cols[:, c, :].rearrange("p (a k) -> p a k", k=P), qst[:, t % 2, h, :], kst[:, 0:qt + 1, h, :],
                                                    start=False, stop=c == hb - 1, skip_group_check=True)
                    last.then_inc(s_full[i], 1)
                pe.wait_ge(s["m4"], t + 1)
                i = begin(t_full, t_free, tuse["M", t])
                nc.tensor.transpose(T[i][:, :].bitcast(bf16)[:, 0:P], mtok[:, t, :, :].rearrange("p g c -> p (g c)"),
                                    idb[:, :]).then_inc(t_full[i], 1)

            def stage_e(t):
                pe.wait_ge(s["maug_ready"], t + 1)
                done(g_free, guse["A", t, 2])
                pe.wait_ge(s["const_ready"], 1)
                blks = blocks_of(t)

                def scores(g):
                    for k, (kt, diagonal) in enumerate(blks):
                        i = begin(s_full, s_free, suse["E", t, g, k])
                        for bank in range(2):
                            cols = SC[i][:, bank * D:(bank + 1) * D].rearrange("p (h q) -> p h q", q=P)
                            if diagonal:
                                nc.tensor.matmul(cols[:, :, :], idb[:, :],
                                                 mask_s[:, 1:2, :].broadcast_to([P, HG // 2, P]), start=True,
                                                 stop=False, skip_group_check=True)
                            for c in range(HG // 2):
                                h = g * HG + bank * (HG // 2) + c
                                last = nc.tensor.matmul(cols[:, c, :], kst[:, kt % QT, h, :], qst[:, t % 2, h, :],
                                                        start=not diagonal, stop=(not diagonal) or c == HG // 2 - 1,
                                                        skip_group_check=True)
                        last.then_inc(s_full[i], 1)

                def values(g):
                    if g % 2 == 0:
                        begin(t_full, t_free, tuse["E", t, g // 2])
                    i = tuse["E", t, g // 2][0]
                    for k in range(len(blks)):
                        done(s_free, suse["E", t, g, k])
                    for quad in range(2):
                        for k, (kt, _) in enumerate(blks):
                            for c in range(4):
                                col = (g % 2) * 2 + quad
                                last = nc.tensor.matmul(T[i][VW * c:VW * (c + 1), col * P:(col + 1) * P],
                                                        vaug[:, kt, g * HG + quad * 4 + c, :],
                                                        pt[:, nblk[t, g, k] % PTN, quad * 4 + c, :],
                                                        start=k == 0, stop=k == len(blks) - 1, skip_group_check=True)
                    last.then_inc(s["pv_done"] if g % 2 == 0 else t_full[i], 1)

                scores(0)
                for g in range(NG):
                    if g + 1 < NG:
                        scores(g + 1)
                    values(g)

            def stage_f(t):
                for half in range(2):
                    done(t_free, tuse["E", t, half])
                    i = begin(t_full, t_free, tuse["F", t, half])
                    for c in range(4):
                        last = nc.tensor.transpose(T[i][:, c * P:(c + 1) * P], osb[:, half, c * P:(c + 1) * P], idf[:, :])
                    last.then_inc(t_full[i], 1)
                for half in range(2):
                    done(t_free, tuse["F", t, half])
                i = begin(t_full, t_free, tuse["FT", t])
                for c in range(KT):
                    last = nc.tensor.transpose(T[i][:, c * P:(c + 1) * P], att[:, c * P:(c + 1) * P], idf[:, :])
                last.then_inc(t_full[i], 1)

            def stage_o(t):
                if t == 0:
                    pe.wait_ge(ld["wo"], 16)
                done(t_free, tuse["FT", t])
                i = begin(g_full, g_free, guse["O", t])
                project(G[i][:, :], attT, wo_s, KT).then_inc(g_full[i], 1)

            def stage_s(b):
                pe.wait_ge(s["q2_ready"], CT * (b + 1))
                pe.wait_ge(s["const_ready"], 1)
                i = begin(g_full, g_free, guse["S", b])
                for kt in range(CT):
                    last = nc.tensor.matmul(G[i][:, :], ones_b[:, :], q2_s[:, b, kt, :], start=kt == 0, stop=kt == CT - 1)
                last.then_inc(g_full[i], 1)

            def stage_g(t):
                pe.wait_ge(s["q1_ready"], t + 1)
                i = begin(t_full, t_free, tuse["G", t])
                for c in range(KT):
                    last = nc.tensor.transpose(T[i][:, :].bitcast(bf16)[:, c * P:(c + 1) * P], q1b[:, c * P:(c + 1) * P], idb[:, :])
                last.then_inc(t_full[i], 1)
                done(t_free, tuse["G", t])
                i = begin(g_full, g_free, guse["G", t])
                project(G[i][:, :], q1T, q2_s[:, t // QT, :, :], CT).then_inc(g_full[i], 1)

            def stage_h(t):
                pe.wait_ge(s["x2_ready"], t + 1)
                i = begin(t_full, t_free, tuse["H", t])
                for c in range(KT):
                    last = nc.tensor.transpose(T[i][:, c * P:(c + 1) * P], x2[:, t, c * P:(c + 1) * P], idf[:, :])
                last.then_inc(t_full[i], 1)
                if t == 0:
                    pe.wait_ge(ld["ar"], 16)
                done(t_free, tuse["H", t])
                i = begin(g_full, g_free, guse["H", t])
                project(G[i][:, 0:E + ER], x2T[:, t % 2, :, :], ar_s, KT).then_inc(g_full[i], 1)

            def stage_i(t):
                if t == 0:
                    pe.wait_ge(ld["wb"], 16)
                    pe.wait_ge(ld["lb"], 16)
                i = begin(g_full, g_free, guse["I", t])
                project(G[i][:, :], x2T[:, t % 2, :, :], wb_s, KT, stop=False)
                pe.wait_ge(s["hw_ready"], t + 1)
                j = begin(t_full, t_free, tuse["I", t])
                nc.tensor.transpose(T[j][:, 0:P], hw[:, :, :].rearrange("p e r -> p (e r)"), idf[:, :]).then_inc(t_full[j], 1)
                done(t_free, tuse["I", t])
                nc.tensor.matmul(G[i][:, :], hwT[:, :], lb_s[:, :], start=False, stop=True).then_inc(g_full[i], 1)

            stages = {"A": stage_a, "B": stage_b, "C": stage_c, "E": stage_e, "F": stage_f, "O": stage_o, "S": stage_s,
                      "G": stage_g, "H": stage_h, "I": stage_i}
            for st, t in ORDER:
                if st in stages:
                    stages[st](t)

        @block.vector
        def _(dve):
            def full(sems, use):
                dve.wait_ge(sems[use[0]], use[1])
                return use[0]

            def tile_stats(n, src):
                nc.vector.bn_stats(stl[:, n, :], src).then_inc(s["stl_ready"], 1)
                count["stl"] += 1
                dve.wait_ge(s["stl_ready"], count["stl"])
                nc.vector.bn_aggr(mvl[:, n, :], stl[:, n, :]).then_inc(s["mvl_ready"], 1)

            def normalise(n, dst, src, signal):
                count["rsl"] += 1
                dve.wait_ge(s["rsl_ready"], count["rsl"])
                nc.vector.tensor_scalar(dst, src, mvl[:, n, 0:1], rsl[:, n, 0:1], ALU.subtract, ALU.mult).then_inc(signal, 1)

            count = {"stl": 0, "rsl": 0}
            last_read = []

            def r_free():
                if last_read:
                    dve.wait_ge(*last_read[-1])


            def stage_a(t):
                if t == 0:
                    dve.wait_ge(ld["scal"], 16)
                    nc.vector.reciprocal(inv_s[:, :], scal_s[:, :].rearrange("p (a c) -> p a c", c=2)[:, :, 0]).then_inc(s["inv_ready"], 1)
                    dve.wait_ge(s["inv_ready"], 1)
                    nc.vector.memset(ones_b[:, :], 1.0)
                    nc.vector.memset(halfs[:, :], -0.5)
                    nc.vector.memset(vaug[:, :, :, DH:VW], 0.0).then_inc(s["vones"], 1)
                    dve.wait_ge(s["vones"], 1)
                    nc.vector.memset(vaug[:, :, :, DH:DH + 1], 1.0).then_inc(s["const_ready"], 1)
                sl = t % 2
                for j in range(2):
                    i = full(g_full, guse["A", t, j])
                    if t >= 1:
                        dve.wait_ge(s["n1_ready"], 2 * (t - 1) + j + 1)
                    nc.vector.tensor_scalar(lin[:, j, :], G[i][:, :], -CLIP, CLIP, ALU.max, ALU.min).then_inc(g_free[i], 1)
                    dve.wait_ge(g_free[i], guse["A", t, j][1])
                    nc.vector.bn_stats(st6[:, j, :], lin[:, j, :]).then_inc(s["st_ready"], 1)
                    dve.wait_ge(s["st_ready"], 2 * t + j + 1)
                    if t >= 2:
                        dve.wait_ge(s["n2_ready"], 2 * (t - 2) + j + 1)
                    nc.vector.bn_aggr(mv[:, sl, j, :], st6[:, j, :]).then_inc(s["mv_ready"], 1)
                i = full(g_full, guse["A", t, 2])
                nc.vector.tensor_scalar(vaug[:, t, :, 0:DH], G[i][:, :].rearrange("p (h d) -> p h d", d=DH),
                                        -CLIP, CLIP, ALU.max, ALU.min).then_inc(g_free[i], 1)

            def stage_n(t):
                sl = t % 2
                for j in range(2):
                    if t >= 1:
                        dve.wait_ge(s["c1_ready"], 2 * (t - 1) + j + 1)
                    dve.wait_ge(s["mv_ready"], 2 * t + j + 1)
                    if t == 0:
                        dve.wait_ge(s["lbias"], 1)
                    nc.vector.scalar_tensor_tensor(nrm[:, j, :], lin[:, j, :], mv[:, sl, j, 0:1], ln_s[:, 2 * j, :],
                                                   ALU.subtract, ALU.mult).then_inc(s["n1_ready"], 1)
                for j in range(2):
                    dve.wait_ge(s["n1_ready"], 2 * t + j + 1)
                    dve.wait_ge(s["rstd_ready"], 2 * t + j + 1)
                    nc.vector.scalar_tensor_tensor(nrm[:, j, :], nrm[:, j, :], rs2[:, sl, j:j + 1], ln_s[:, 2 * j + 1, :],
                                                   ALU.mult, ALU.add).then_inc(s["n2_ready"], 1)
                for j in range(2):
                    c1at, c2at, c3at = (2, 0, 1) if j == 0 else (0, 3, 4)
                    v = nrm[:, j, :].rearrange("p (h d) -> p h d", d=DH)
                    r = res[:, j, :].rearrange("p (h d) -> p h d", d=DH)
                    dve.wait_ge(s["c1_ready"], 2 * t + j + 1)
                    nc.vector.tensor_tensor(r, v, stk[:, j, :, c1at * DH:(c1at + 1) * DH], ALU.subtract).then_inc(s["r_ready"], 1)
                for j in range(2):
                    c1at, c2at, c3at = (2, 0, 1) if j == 0 else (0, 3, 4)
                    r = res[:, j, :].rearrange("p (h d) -> p h d", d=DH)
                    dve.wait_ge(s["c2_ready"], 2 * t + j + 1)
                    nc.vector.tensor_tensor(stk[:, j, :, c3at * DH:(c3at + 1) * DH], r,
                                            stk[:, j, :, c2at * DH:(c2at + 1) * DH], ALU.subtract).then_inc(s["c3_ready"], 1)

            def stage_b(t):
                if t >= 2:
                    scores_done(dve, t - 2)
                for g in range(NG):
                    i = full(t_full, tuse["B", t, 1, g])
                    nc.vector.tensor_copy(qst[0:PR, t % 2, g * HG:(g + 1) * HG, :],
                                          T[i][:, :].bitcast(bf16)[0:PR, :].rearrange("p (h q) -> p h q", q=P)).then_inc(t_free[i], 1)

            def stage_c(t):
                qt = t % QT
                per = HG // (1 + qt)
                for u in range(H // per):
                    i = full(s_full, suse["C", t, u])
                    nc.vector.tensor_reduce(mx[:, u * per:(u + 1) * per],
                                            SC[i][:, :].rearrange("p (h k) -> p h k", h=per), AX.X, ALU.max).then_inc(s_free[i], 1)
                dve.wait_ge(s_free[i], suse["C", t, u][1])
                dve.wait_ge(s_free[1 - i], suse["C", t, u - 1][1])
                if t == 0:
                    dve.wait_ge(ld["mcols"], 16 * TILES)
                m_v = mx[:, :].rearrange("p (g c) -> p g c", c=HG)
                d_v = md[:, :].rearrange("p (g c) -> p g c", c=HG)
                nc.vector.tensor_scalar(mtok[:, t, :, 0:HG], m_v, -1.0, None, ALU.mult).then_inc(s["m1"], 1)
                dve.wait_ge(s["m1"], t + 1)
                nc.vector.scalar_tensor_tensor(d_v, m_v, -1.0, mtok[:, t, :, 0:HG], ALU.mult, ALU.subtract).then_inc(s["m2"], 1)
                dve.wait_ge(s["m2"], t + 1)
                nc.vector.tensor_copy(mtok[:, t, :, HG:2 * HG], d_v).then_inc(s["m3"], 1)
                dve.wait_ge(s["m3"], t + 1)
                nc.vector.tensor_tensor(mtok[:, t, :, 2 * HG:3 * HG], d_v, mtok[:, t, :, HG:2 * HG], ALU.subtract).then_inc(s["m4"], 1)
                i = full(t_full, tuse["M", t])
                nc.vector.tensor_copy(mT[:, :], T[i][:, :].bitcast(bf16)[:, 0:P]).then_inc(t_free[i], 1)
                dve.wait_ge(t_free[i], tuse["M", t][1])
                for g in range(NG):
                    last = nc.vector.tensor_copy(qst[P - AUG:P, t % 2, g * HG:(g + 1) * HG, :],
                                                 mT[AUG * g:AUG * (g + 1), :].unsqueeze(1).broadcast_to([AUG, HG, P]))
                last.then_inc(s["maug_ready"], 1)

            def stage_e(t):
                for half in range(2):
                    i = full(t_full, tuse["E", t, half])
                    if t >= 1:
                        dve.wait_ge(t_full[tuse["F", t - 1, half][0]], tuse["F", t - 1, half][1])
                    nc.vector.tensor_copy(osb[:, half, :], T[i][:, :]).then_inc(t_free[i], 1)

            def stage_f(t):
                for half in range(2):
                    i = full(t_full, tuse["F", t, half])
                    o = T[i][:, :].rearrange("p (h c) -> p h c", c=VW)
                    nc.vector.reciprocal(rsum[:, half, :], o[:, :, DH]).then_inc(s["rsum_ready"], 1)
                    dve.wait_ge(s["rsum_ready"], 2 * t + half + 1)
                    if t >= 1:
                        dve.wait_ge(t_full[tuse["FT", t - 1][0]], tuse["FT", t - 1][1])
                    nc.vector.tensor_tensor(att[:, half * 256:(half + 1) * 256].rearrange("p (h d) -> p h d", d=DH),
                                            o[:, :, 0:DH], rsum[:, half, :].unsqueeze(2).broadcast_to([P, H // 2, DH]),
                                            ALU.mult).then_inc(t_free[i], 1)

            def stage_o(t):
                i = full(g_full, guse["O", t])
                if t == 0:
                    dve.wait_ge(ld["xrow"], 16)
                r_free()
                nc.vector.tensor_tensor(r1[:, :], G[i][:, :], x_s[:, t, :], ALU.add).then_inc(g_free[i], 1)
                dve.wait_ge(g_free[i], guse["O", t][1])
                tile_stats(0, r1[:, :])
                normalise(0, x1[:, t, :], r1[:, :], s["x1_ready"])
                dve.wait_ge(s["x1_ready"], t + 1)
                nc.vector.tensor_scalar(qd[:, :], x1[:, t, :], inv_s[:, 0:1], scal_s[:, 1:2], ALU.mult, ALU.add).then_inc(s["qd1"], 1)
                dve.wait_ge(s["qd1"], t + 1)
                nc.vector.tensor_scalar(qd[:, :], qd[:, :], QMAX, ROUND, ALU.min, ALU.add).then_inc(s["qd2"], 1)
                dve.wait_ge(s["qd2"], t + 1)
                if t >= 1:
                    dve.wait_ge(s["rowsum_ready"], t)
                    dve.wait_ge(t_full[tuse["G", t - 1][0]], tuse["G", t - 1][1])
                nc.vector.tensor_scalar(q1b[:, :], qd[:, :], ROUND, -(ROUND + CENTRE), ALU.max, ALU.add).then_inc(s["q1_ready"], 1)
                last_read.append((s["q1_ready"], t + 1))

            def stage_s(b):
                if b == 0:
                    z = scal_s[:, :].rearrange("p (a c) -> p a c", c=2)
                    nc.vector.tensor_scalar(a12[:, :], z[:, :, 1], -1.0, CENTRE, ALU.mult, ALU.add).then_inc(s["sc1"], 1)
                    nc.vector.tensor_tensor(s12[:, :], scal_s[:, 0:1], scal_s[:, 2:3], ALU.mult).then_inc(s["sc1"], 1)
                    dve.wait_ge(s["sc1"], 2)
                    nc.vector.tensor_scalar(kaa[:, :], a12[:, 0:1], a12[:, 1:2], float(CTX), ALU.mult, ALU.mult).then_inc(s["sc2"], 1)
                    dve.wait_ge(s["sc2"], 1)
                i = full(g_full, guse["S", b])
                nc.vector.tensor_scalar(colc[:, b, :], G[i][:, :], a12[:, 0:1], kaa[:, :], ALU.mult, ALU.add).then_inc(g_free[i], 1)

            def stage_g(t):
                b = t // QT
                dve.wait_ge(s["rowsum_ready"], t + 1)
                nc.vector.tensor_tensor(arq[:, :], rsq[:, :], a12[:, 1:2], ALU.mult).then_inc(s["arq_ready"], 1)
                dve.wait_ge(s["arq_ready"], t + 1)
                i = full(g_full, guse["G", t])
                dve.wait_ge(g_free[guse["S", b][0]], guse["S", b][1])
                r_free()
                nc.vector.scalar_tensor_tensor(r2[:, :], G[i][:, :], arq[:, :], colc[:, b, :], ALU.add, ALU.add).then_inc(g_free[i], 1)
                dve.wait_ge(g_free[i], guse["G", t][1])
                nc.vector.scalar_tensor_tensor(r2[:, :], r2[:, :], s12[:, :], x1[:, t, :], ALU.mult, ALU.add).then_inc(s["r2_ready"], 1)
                dve.wait_ge(s["r2_ready"], t + 1)
                tile_stats(1, r2[:, :])
                normalise(1, x2[:, t, :], r2[:, :], s["x2_ready"])
                last_read.append((s["x2_ready"], t + 1))

            def stage_h(t):
                i = full(g_full, guse["H", t])
                sl = t % 2
                nc.vector.tensor_copy(lg[:, sl, :], G[i][:, 0:E + ER]).then_inc(g_free[i], 1)
                dve.wait_ge(g_free[i], guse["H", t][1])
                nc.vector.max(top[:, :], lg[:, sl, 0:E]).then_inc(s["top_ready"], 1)
                dve.wait_ge(s["top_ready"], t + 1)
                if t >= 1:
                    dve.wait_ge(s["ex_ready"], t)
                nc.vector.tensor_tensor(dl[:, :], top[:, 1:2], top[:, 0:1], ALU.subtract).then_inc(s["dl_ready"], 1)
                nc.vector.max_index(idx[:, :], top[:, :], lg[:, sl, 0:E]).then_inc(s["idx_ready"], 1)
                dve.wait_ge(s["idx_ready"], t + 1)
                nc.vector.tensor_copy(idxf[:, :], idx[:, 0:2]).then_inc(s["idxf_ready"], 1)
                dve.wait_ge(s["ex_ready"], t + 1)
                nc.vector.tensor_scalar(den[:, :], ex[:, :], 1.0, 1.0 / LORA_SCALE, ALU.add, ALU.mult).then_inc(s["den_ready"], 1)
                dve.wait_ge(s["den_ready"], t + 1)
                nc.vector.reciprocal(w01[:, 0:1], den[:, :]).then_inc(s["w0_ready"], 1)
                dve.wait_ge(s["w0_ready"], t + 1)
                nc.vector.tensor_tensor(w01[:, 1:2], w01[:, 0:1], ex[:, :], ALU.mult).then_inc(s["w1_ready"], 1)
                dve.wait_ge(s["w1_ready"], t + 1)
                dve.wait_ge(s["idxf_ready"], t + 1)
                for j in range(2):
                    nc.vector.tensor_scalar(wsel[:, j, :], iota_s[:, :], idxf[:, j:j + 1], w01[:, j:j + 1],
                                            ALU.is_equal, ALU.mult).then_inc(s["ws0"], 1)
                dve.wait_ge(s["ws0"], 2 * t + 2)
                nc.vector.tensor_tensor(wsel[:, 0, :], wsel[:, 0, :], wsel[:, 1, :], ALU.add).then_inc(s["wsel_ready"], 1)
                dve.wait_ge(s["wsel_ready"], t + 1)
                if t >= 1:
                    dve.wait_ge(t_full[tuse["I", t - 1][0]], tuse["I", t - 1][1])
                nc.vector.tensor_tensor(hw[:, :, :], lg[:, sl, E:E + ER].rearrange("p (e r) -> p e r", r=R),
                                        wsel[:, 0, :].unsqueeze(2).broadcast_to([P, E, R]), ALU.mult).then_inc(s["hw_ready"], 1)

            def stage_i(t):
                i = full(g_full, guse["I", t])
                dve.wait_ge(s["xb_ready"], t + 1)
                r_free()
                nc.vector.tensor_tensor(r3[:, :], G[i][:, :], xb[:, t % 2, :], ALU.add).then_inc(g_free[i], 1)
                dve.wait_ge(g_free[i], guse["I", t][1])
                tile_stats(2, r3[:, :])
                normalise(2, x3[:, t, :], r3[:, :], s["x3_ready"])
                last_read.append((s["x3_ready"], t + 1))

            stages = {"A": stage_a, "N": stage_n, "B": stage_b, "C": stage_c, "E": stage_e, "F": stage_f, "O": stage_o,
                      "S": stage_s, "G": stage_g, "H": stage_h, "I": stage_i}
            for st, t in ORDER:
                stages[st](t)

        @block.scalar
        def _(act):
            def values_done(m):
                t, g = exp_tiles[m // NG], m % NG
                if g % 2 == 0:
                    act.wait_ge(s["pv_done"], m // 2 + 1)
                else:
                    full(t_full, tuse["E", t, g // 2])

            def full(sems, use):
                act.wait_ge(sems[use[0]], use[1])
                return use[0]

            def stage_n(t):
                for j in range(2):
                    act.wait_ge(s["n2_ready"], 2 * t + j + 1)
                    if t >= 1:
                        use = tuse["B", t - 1, j, NG - 1]
                        act.wait_ge(t_full[use[0]], use[1])
                        use = tuse["B", t - 1, j, NG - 2]
                        act.wait_ge(t_full[use[0]], use[1])
                    at = 2 if j == 0 else 0
                    nc.scalar.activation(
                        stk[:, j, :, at * DH:(at + 3) * DH].rearrange("p h (a d) -> p h a d", d=DH),
                        nrm[:, j, :].rearrange("p (h d) -> p h d", d=DH).unsqueeze(2).broadcast_to([P, H, 3, DH]),
                        ACT.Copy).then_inc(s["c1_ready"], 1)
                for j in range(2):
                    act.wait_ge(s["r_ready"], 2 * t + j + 1)
                    at, step = (0, 5) if j == 0 else (3, 2)
                    parts = stk[:, j, :, :].rearrange("p h (a d) -> p h a d", d=DH)
                    nc.scalar.activation(
                        parts[:, :, at:at + step + 1:step, :],
                        res[:, j, :].rearrange("p (h d) -> p h d", d=DH).unsqueeze(2).broadcast_to([P, H, 2, DH]),
                        ACT.Copy).then_inc(s["c2_ready"], 1)

            def stage_b(t):
                if t >= QT:
                    scores_done(act, t - t % QT - 1)
                for g in range(NG):
                    i = full(t_full, tuse["B", t, 0, g])
                    nc.scalar.activation(kst[0:PR, t % QT, g * HG:(g + 1) * HG, :],
                                         T[i][:, :].bitcast(bf16)[0:PR, :].rearrange("p (h q) -> p h q", q=P),
                                         ACT.Copy).then_inc(t_free[i], 1)

            def stage_e(t):
                for g in range(NG):
                    for k in range(len(blocks_of(t))):
                        i = full(s_full, suse["E", t, g, k])
                        n = nblk[t, g, k]
                        if n >= PTN:
                            values_done(grp_of[n - PTN])
                        nc.scalar.activation(pt[:, n % PTN, :, :].rearrange("p h q -> p (h q)"), SC[i][:, :], ACT.Exp).then_inc(s_free[i], 1)

            def stage_f(t):
                i = full(t_full, tuse["FT", t])
                if t >= 1:
                    use = guse["O", t - 1]
                    act.wait_ge(g_full[use[0]], use[1])
                nc.scalar.activation(attT[:, :, :].rearrange("p a b -> p (a b)"), T[i][:, :], ACT.Copy).then_inc(t_free[i], 1)

            def stage_g(t):
                i = full(t_full, tuse["G", t])
                if t >= 1:
                    use = guse["G", t - 1]
                    act.wait_ge(g_full[use[0]], use[1])
                nc.scalar.activation(q1T[:, :, :].rearrange("p a b -> p (a b)"), T[i][:, :].bitcast(bf16)[:, 0:D], ACT.Copy).then_inc(t_free[i], 1)
                if t >= 1:
                    act.wait_ge(s["arq_ready"], t)
                nc.scalar.activation(junk[:, :], q1b[:, :], ACT.Copy, accum_out=rsq[:, :]).then_inc(s["rowsum_ready"], 1)

            def stage_h(t):
                i = full(t_full, tuse["H", t])
                nc.scalar.activation(x2T[:, t % 2, :, :].rearrange("p a b -> p (a b)"), T[i][:, :], ACT.Copy).then_inc(t_free[i], 1)
                act.wait_ge(s["dl_ready"], t + 1)
                if t >= 1:
                    act.wait_ge(s["w1_ready"], t)
                nc.scalar.activation(ex[:, :], dl[:, :], ACT.Exp).then_inc(s["ex_ready"], 1)

            def stage_i(t):
                i = full(t_full, tuse["I", t])
                if t >= 1:
                    use = guse["I", t - 1]
                    act.wait_ge(g_full[use[0]], use[1])
                nc.scalar.activation(hwT[:, :], T[i][:, 0:P], ACT.Copy).then_inc(t_free[i], 1)

            stages = {"N": stage_n, "B": stage_b, "E": stage_e, "F": stage_f, "G": stage_g, "H": stage_h, "I": stage_i}
            for st, t in ORDER:
                if st in stages:
                    stages[st](t)

        @block.gpsimd
        def _(pool):
            scale = DH ** -0.5

            def rstd(dst, tmp, var, n, ready, mid):
                nc.gpsimd.tensor_scalar(tmp, var, EPS, None, ALU.add).then_inc(s[mid], 1)
                count[mid] += 1
                pool.wait_ge(s[mid], count[mid])
                nc.gpsimd.tensor_tensor(dst, tmp, halfs[:, 0:n], ALU.pow).then_inc(s[ready], 1)
                count[ready] += 1

            count = {"ve_ready": 0, "rstd_ready": 0, "vel_ready": 0, "rsl_ready": 0}

            def stage_a(t):
                sl = t % 2
                if t == 0:
                    pool.wait_ge(ld["qaug"], 16)
                    pool.wait_ge(ld["ln"], 16)
                    nc.gpsimd.tensor_scalar(ln_s[:, 2:4, :], ln_s[:, 2:4, :], scale, None, ALU.mult).then_inc(s["lbias"], 1)
                    pool.wait_ge(s["lbias"], 1)
                    pool.wait_ge(s["const_ready"], 1)
                for j in range(2):
                    pool.wait_ge(s["mv_ready"], 2 * t + j + 1)
                    rstd(rs2[:, sl, j:j + 1], ve2[:, j:j + 1], mv[:, sl, j, 1:2], 1, "rstd_ready", "ve_ready")

            def stage_b(t):
                if t >= 2:
                    scores_done(pool, t - 2)
                for signal in ("rstd_ready", "rsl_ready", "q2_ready", "xb_ready"):
                    if count.get(signal, 0) > 0:
                        pool.wait_ge(s[signal], count[signal])
                nc.gpsimd.tensor_scalar(qst[P - AUG:P, t % 2, :, :],
                                        qaug_s[P - AUG:P, t % QT, :].unsqueeze(1).broadcast_to([AUG, H, P]),
                                        1.0, None, ALU.mult).then_inc(s["qaug_ready"], 1)
                pool.wait_ge(s["qaug_ready"], t + 1)

            def stage_o(t):
                ln_rstd(0)

            def ln_rstd(n):
                count["mvl"] = count.get("mvl", 0) + 1
                pool.wait_ge(s["mvl_ready"], count["mvl"])
                rstd(rsl[:, n, :], vel[:, n, :], mvl[:, n, 1:2], 1, "rsl_ready", "vel_ready")

            def stage_g(t):
                ln_rstd(1)
                pool.wait_ge(s["x2_ready"], t + 1)
                if t >= 2:
                    pool.wait_ge(g_free[guse["I", t - 2][0]], guse["I", t - 2][1])
                nc.gpsimd.tensor_tensor(xb[:, t % 2, :], x2[:, t, :], ln_s[:, 4, :], ALU.add).then_inc(s["xb_ready"], 1)
                count["xb_ready"] = t + 1

            def stage_i(t):
                ln_rstd(2)

            def quantise_context(c):
                b, kt = c // CT, c % CT
                if kt == 0:
                    pool.wait_ge(ld["ctx"], 16 * (b + 1))
                    pool.wait_ge(s["inv_ready"], 1)
                v = ctx_s[:, kt, :]
                nc.gpsimd.tensor_scalar(v, v, inv_s[:, 1:2], scal_s[:, 3:4], ALU.mult, ALU.add).then_inc(s["q2a"], 1)
                pool.wait_ge(s["q2a"], c + 1)
                nc.gpsimd.tensor_scalar(v, v, QMAX, ROUND, ALU.min, ALU.add).then_inc(s["q2b"], 1)
                pool.wait_ge(s["q2b"], c + 1)
                nc.gpsimd.tensor_scalar(q2_s[:, b, kt, :], v, ROUND, -(ROUND + CENTRE), ALU.max, ALU.add).then_inc(s["q2_ready"], 1)
                count["q2_ready"] = c + 1

            stages = {"A": stage_a, "B": stage_b, "O": stage_o, "G": stage_g, "I": stage_i}
            for st, t in ORDER:
                if st in stages:
                    stages[st](t)
                if (st, t) in (("A", 2), ("A", 3)):
                    for c in range(CT):
                        quantise_context((t - 2) * CT + c)


def three_parts(a):
    bfloat16 = mybir.dt.np(mybir.dt.bfloat16)
    a = a.astype(np.float64)
    hi = a.astype(np.float32).astype(bfloat16)
    mid = (a - hi.astype(np.float64)).astype(np.float32).astype(bfloat16)
    lo = (a - hi.astype(np.float64) - mid.astype(np.float64)).astype(np.float32).astype(bfloat16)
    return hi, mid, lo


def constants():
    bfloat16 = mybir.dt.np(mybir.dt.bfloat16)
    ident = np.eye(P, dtype=np.float32)
    i = np.arange(P)
    mask = np.where(i[:, None] >= i[None, :], 0.0, MASKED).astype(np.float32)
    masks = np.stack([mask, mask.T], axis=1).astype(bfloat16)
    slopes = (1.0 / np.power(np.float32(2.0), np.arange(1, H + 1, dtype=np.float32) * np.float32(8.0 / H))).astype(np.float32)
    pos = np.arange(S)
    kaug = np.zeros((AUG, QT, H, P), dtype=bfloat16)
    rise = three_parts(slopes[:, None].astype(np.float64) * pos[None, :])
    fall = three_parts(-slopes)
    for h in range(H):
        for part in range(3):
            kaug[part * HG + h % HG, :, h, :] = 1.0
            kaug[3 * HG + part, :, h, :] = rise[part][h].reshape(QT, P)
            kaug[3 * HG + 3 + part, :, h, :] = fall[part][h]
    qaug = np.zeros((AUG, QT, P), dtype=bfloat16)
    qaug[3 * HG:3 * HG + 3] = 1.0
    qaug[3 * HG + 3:3 * HG + 6] = pos.reshape(QT, P)[None]
    mcols = np.zeros((QT, P, H // HG, AUG), dtype=bfloat16)
    mcols[:] = np.transpose(qaug, (1, 2, 0))[:, :, None, :]
    iota = np.broadcast_to(np.arange(E, dtype=np.float32), (P, E)).copy()
    return ident, ident.astype(bfloat16), masks, kaug, qaug, mcols, iota


def kernel(**inputs):
    import concourse.bacc as _bacc
    from concourse.bass_utils import run_bass_kernel_spmd as _run

    f = {k: np.asarray(v) for k, v in inputs.items()}

    def rows(w, n):
        return np.ascontiguousarray(w.reshape(-1, P, n).transpose(1, 0, 2))

    x = f["x"].reshape(B * S, D)
    xT = np.ascontiguousarray(x.reshape(TILES, P, KT, P).transpose(0, 3, 2, 1))
    xrow = np.ascontiguousarray(x.reshape(TILES, P, D).transpose(1, 0, 2))
    wq, wk, wv = f["L0_attn_w_qkv"].reshape(3, D, D)
    wqkvT = np.stack([rows(w.T, D) for w in (wk, wq, wv)])
    ln = np.stack([f["L0_attn_k_ln_w"], f["L0_attn_k_ln_b"], f["L0_attn_q_ln_w"], f["L0_attn_q_ln_b"], f["L0_ffn_b_base"]])
    ln = np.ascontiguousarray(np.broadcast_to(ln, (P, 5, D)))
    woT = rows(f["L0_attn_w_out"].T, D)
    ctx4 = np.stack([rows(f["ctx_4096"][b], D) for b in range(B)])
    scal = np.concatenate([f["L0_xattn_x1_scale"], f["L0_xattn_x1_zp"], f["L0_xattn_x2_scale"], f["L0_xattn_x2_zp"]])
    scal = np.ascontiguousarray(np.broadcast_to(scal, (P, 4)))
    wbT = rows(f["L0_ffn_W_base"].T, D)
    arT = rows(np.concatenate([f["L0_ffn_W_router"], f["L0_ffn_A"].reshape(ER, D)]).T, E + ER)
    loraB = np.ascontiguousarray(f["L0_ffn_B"].transpose(0, 2, 1).reshape(ER, D))
    ident, identb, masks, kaug, qaug, mcols, iota = constants()

    nc = _bacc.Bacc("TRN2", target_bir_lowering=False, num_devices=1)
    arrays, args = {}, []
    for name, a in dict(xT=xT, xrow=xrow, wqkvT=wqkvT, ln=ln, woT=woT, ctx4=ctx4, scal=scal, wbT=wbT, arT=arT, loraB=loraB,
                        identf=ident, identb=identb, maskc=masks, kaug=kaug, qaug=qaug, mcols=mcols, iota=iota).items():
        a = np.ascontiguousarray(a)
        arrays[name + "_dram"] = a
        args.append(nc.dram_tensor(name + "_dram", a.shape, mybir.dt.from_np(a.dtype), kind="ExternalInput").ap())
    out = nc.dram_tensor("out_dram", (TILES, P, D), mybir.dt.float32, kind="ExternalOutput").ap()
    build(nc, *args, out)
    r = _run(nc, [arrays], core_ids=[0])
    return r.results[0]["out_dram"].reshape(B, S, D)
```

```python
import numpy as np
import concourse.bass as bass
from concourse import mybir
from contextlib import ExitStack

P = 128
B, S, D = 2, 256, 512
TILES = B * S // P
QT = S // P
KT = D // P
H = 32
DH = D // H
PARTS = 6
PR = PARTS * DH
AUG = 32
HG = 8
NG = H // HG
VW = 32
E = 8
R = 16
ER = E * R
CTX = 512
CT = CTX // P
CLIP = 8.0
EPS = 1e-5
LORA_SCALE = 2.0
MASKED = -1e30
QMAX = 255.0
CENTRE = 128.0
ROUND = 1.5 * 2.0 ** 23

ORDER = [(w[0], int(w[1]), w[2:]) for w in """L0 A0k N0k A0q N0q D0k D0q A0v W0k W0q A1k A1q B0 N1k N1q A1v D1k C00 D1q C01 W1q W1k A2k C02 C03 M0 A2q T0 U0 A2v E00 B1 E01 V00 V01 E02 E03 V02 N2k N2q F00 D2kq V03 A3k C101 F01 C123 Z0 C14 C15 A3q W2kq C16 P0 C17 M1 A3v T1 U1 O0 Q0 E10 E11 V10 E12 V11 E13 S0 V12 V13 B2 N3k N3q C201 D3kq C223 W3kq G0 M2 F10 T2 U2 F11 E20 X0 E21 V20 P1 E22 V21 O1 E23 F20 V22 Y0 V23 Q1 B3 F21 C30 G1 C31 H0 C32 C3345 C36 P2 C37 R0 M3 O2 Z1 T3 U3 I0 E30 X1 E31 S1 J0 Y1 V30 V31 E32 F30 Q2 E33 H1 V32 V33 G2 R1 F31 I1 X2 P3 J1 Y2 O3 H2 R2 Q3 I2 G3 X3 J2 Y3 H3 R3 I3 J3""".split()]


def bank_uses(keys, slots):
    return {key: (i % slots, i // slots + 1) for i, key in enumerate(keys)}


def blocks_of(t):
    return [(k, k == t) for k in range(t - t % QT, t + 1)]


def build(nc, xT, xrow, wqkvT, ln, woT, ctx4, scal, wbT, arT, loraB, identf, identb, maskc, kaug, qaug, mcols, iota, out):
    fp32, bf16, u32 = mybir.dt.float32, mybir.dt.bfloat16, mybir.dt.uint32
    ALU = mybir.AluOpType
    ACT = mybir.ActivationFunctionType
    AX = mybir.AxisListType

    ctx = ExitStack()
    with ctx:
        def sb(name, shape, dt=fp32):
            return ctx.enter_context(nc.sbuf_tensor(name, shape, dt))

        def pb(name, shape, dt=fp32):
            return ctx.enter_context(nc.psum_tensor(name, shape, dt))

        def sem(name):
            return ctx.enter_context(nc.semaphore(name))

        xT_s = sb("xT_s", [P, TILES, KT, P])
        x_s = sb("x_s", [P, TILES, D])
        wqkv_s = sb("wqkv_s", [P, 3, KT, D])
        ln_s = sb("ln_s", [P, 5, D])
        wo_s = sb("wo_s", [P, KT, D])
        ctx_s = sb("ctx_s", [P, CT, D])
        q2_s = sb("q2_s", [P, 2, CT, D], bf16)
        wb_s = sb("wb_s", [P, KT, D])
        ar_s = sb("ar_s", [P, KT, E + ER])
        lb_s = sb("lb_s", [ER, D])
        idf = sb("idf", [P, P])
        idb = sb("idb", [P, P], bf16)
        mask_s = sb("mask_s", [P, 2, P], bf16)
        ones_b = sb("ones_b", [P, P], bf16)
        iota_s = sb("iota_s", [P, E])
        scal_s = sb("scal_s", [P, 4])
        a12 = sb("a12", [P, 2])
        inv_s = sb("inv_s", [P, 2])
        s12 = sb("s12", [P, 1])
        kaa = sb("kaa", [P, 1])
        halfs = sb("halfs", [P, 2])
        kst = sb("kst", [P, QT, H, P], bf16)
        qst = sb("qst", [P, 2, H, P], bf16)
        vaug = sb("vaug", [P, TILES, H, VW])
        lin = sb("lin", [P, 2, D])
        nrm = sb("nrm", [P, 2, D])
        stk = sb("stk", [P, 2, H, PR], bf16)
        st6 = sb("st6", [P, 2, 6])
        mv = sb("mv", [P, 2, 2, 2])
        rs2 = sb("rs2", [P, 2, 2])
        ve2 = sb("ve2", [P, 2])
        mx = sb("mx", [P, H])
        md = sb("md", [P, H])
        mtok = sb("mtok", [P, TILES, NG, AUG], bf16)
        mT = sb("mT", [P, P], bf16)
        PTN = 4
        pt = sb("pt", [P, PTN, HG, P])
        osb = sb("osb", [P, 2, D])
        rsum = sb("rsum", [P, 2, H // 2])
        att = sb("att", [P, D])
        attT = sb("attT", [P, KT, P])
        r1, r2, r3 = [sb(f"r{n}", [P, D]) for n in (1, 2, 3)]
        qd = r1
        x1 = x2 = x3 = x_s
        stl = sb("stl", [P, 3, 6])
        mvl = sb("mvl", [P, 3, 2])
        vel = sb("vel", [P, 3, 1])
        rsl = sb("rsl", [P, 3, 1])
        q1b = sb("q1b", [P, D], bf16)
        junk = sb("junk", [P, D], bf16)
        rsq = sb("rsq", [P, 1])
        arq = sb("arq", [P, 1])
        q1T = sb("q1T", [P, KT, P], bf16)
        colc = sb("colc", [P, 2, D])
        xb = sb("xb", [P, 2, D])
        x2T = sb("x2T", [P, 2, KT, P])
        lg = sb("lg", [P, 2, E + ER])
        top = sb("top", [P, 8])
        idx = sb("idx", [P, 8], u32)
        idxf = sb("idxf", [P, 2])
        dl = sb("dl", [P, 1])
        ex = sb("ex", [P, 1])
        den = sb("den", [P, 1])
        w01 = sb("w01", [P, 2])
        wsel = sb("wsel", [P, 2, E])
        hw = sb("hw", [P, E, R])
        hwT = sb("hwT", [P, P])

        G = [pb(f"G{i}", [P, D]) for i in range(2)]
        T = [pb(f"T{i}", [P, D]) for i in range(2)]
        SC = [pb(f"SC{i}", [P, 2 * D]) for i in range(2)]
        gkeys, tkeys, skeys = [], [], []
        for st, t, which in ORDER:
            if st == "A":
                gkeys += [("A", t, "kqv".index(c)) for c in which]
            if st == "B":
                skeys += [("B", t, half) for half in range(2)]
                tkeys += [("B", t, g) for g in range(NG)]
            if st == "C":
                skeys += [("C", t, int(g)) for g in which]
            if st == "E":
                skeys += [("E", t, int(which), k) for k in range(len(blocks_of(t)))]
            if st == "V" and which in "02":
                tkeys += [("E", t, int(which) // 2)]
            if st == "F":
                tkeys += [("F", t, int(which))]
            if st == "T":
                tkeys += [("M", t)]
            if st in "PGHI":
                tkeys += [(st, t)]
            if st in "OSXRI":
                gkeys += [(st, t)]
        guse, tuse, suse = bank_uses(gkeys, 2), bank_uses(tkeys, 2), bank_uses(skeys, 2)
        g_full, g_free = [sem(f"g_full{i}") for i in range(2)], [sem(f"g_free{i}") for i in range(2)]
        t_full, t_free = [sem(f"t_full{i}") for i in range(2)], [sem(f"t_free{i}") for i in range(2)]
        s_full, s_free = [sem(f"s_full{i}") for i in range(2)], [sem(f"s_free{i}") for i in range(2)]

        ld_x = [sem(f"ld_x{t}") for t in range(TILES)]
        ld_qaug = [sem(f"ld_qaug{t}") for t in range(TILES)]
        ld_ln = {what: sem("ld_ln_" + what) for what in ("k", "q", "base")}
        ld_wk = [sem(f"ld_wk{kt}") for kt in range(KT)]
        ld_w = [sem(f"ld_w{j}") for j in range(3)]
        names = ("id mask kaug qaug mcols xrow wo ctx scal wb ar lb iota").split()
        ld = {n: sem("ld_" + n) for n in names}

        prod = ("ones_ready const_ready lin_ready v_ready st_ready mv_ready ve_ready rstd_ready n1_ready n2_ready c1_ready r_ready c2_ready "
                "c3_ready stack_ready vones qaug_ready max_ready m1 m2 m3 m4 mT_ready maug_ready exp_ready pv_done "
                "o_ready rsum_ready att_ready attT_ready r1_ready stl_ready mvl_ready vel_ready rsl_ready x1_ready "
                "qd1 qd2 qd3 q1_ready rowsum_ready arq_ready q1T_ready col_ready t1_ready r2_ready x2_ready "
                "xb_ready x2T_ready lg_ready top_ready idx_ready idxf_ready dl_ready ex_ready den_ready w_ready w0_ready w1_ready "
                "ws0 ws1 wsel_ready hw_ready hwT_ready r3_ready x3_ready out_done inv_ready q2a q2b q2_ready sc1 sc2 "
                "qln_scaled").split()
        s = {n: sem(n) for n in prod}

        def scores_done(eng, t):
            for g in range(NG - 2, NG):
                for k in range(len(blocks_of(t))):
                    eng.wait_ge(s_full[suse["E", t, g, k][0]], suse["E", t, g, k][1])

        block = ctx.enter_context(nc.Block())

        @block.sync
        def _(sp):
            def load(dst, src, signal):
                sp.dma_start(dst, src).then_inc(signal, 16)

            def load_ln(what, first, count):
                load(ln_s[:, first:first + count, :], ln[:, first:first + count, :].broadcast_to([P, count, D]), ld_ln[what])

            load(xT_s[:, 0, :, :], xT[0], ld_x[0])
            for kt in range(KT):
                load(wqkv_s[:, 0, kt, :], wqkvT[0, :, kt, :], ld_wk[kt])
            load(wqkv_s[:, 1, :, :], wqkvT[1], ld_w[1])
            load_ln("k", 0, 2)
            load_ln("q", 2, 2)
            load(wqkv_s[:, 2, :, :], wqkvT[2], ld_w[2])
            load(scal_s[:, :], scal, ld["scal"])
            load(idf[:, :], identf, ld["id"])
            load(idb[:, :], identb, ld["id"])
            load(mask_s[:, :, :], maskc, ld["mask"])
            for t in range(2):
                load(qst[P - AUG:P, t, :, :], qaug[t % QT], ld_qaug[t])
            load(xT_s[:, 1, :, :], xT[1], ld_x[1])
            load(kst[P - AUG:P, :, :, :], kaug, ld["kaug"])
            for t in range(TILES):
                load(mtok[:, t, :, :], mcols[t % QT], ld["mcols"])
            for t in range(2, TILES):
                load(xT_s[:, t, :, :], xT[t], ld_x[t])
            load(iota_s[:, :], iota, ld["iota"])
            load(x_s[:, :, :], xrow, ld["xrow"])
            load(wo_s[:, :, :], woT, ld["wo"])
            load(ctx_s[:, :, :], ctx4[0], ld["ctx"])
            load(ar_s[:, :, :], arT, ld["ar"])
            load(wb_s[:, :, :], wbT, ld["wb"])
            load_ln("base", 4, 1)
            load(lb_s[:, :], loraB, ld["lb"])
            sp.wait_ge(s["q2_ready"], 1)
            load(ctx_s[:, :, :], ctx4[1], ld["ctx"])
            for t in range(2, TILES):
                scores_done(sp, t - 2)
                load(qst[P - AUG:P, t % 2, :, :], qaug[t % QT], ld_qaug[t])
            for t in range(TILES):
                sp.wait_ge(s["x3_ready"], t + 1)
                sp.dma_start(out[t], x3[:, t, :]).then_inc(s["out_done"], 16)
            sp.wait_ge(s["out_done"], 16 * TILES)

        nblk, grp_of = {}, []
        for st, t, which in ORDER:
            if st == "E":
                for k in range(len(blocks_of(t))):
                    nblk[t, int(which), k] = len(grp_of)
                    grp_of.append((t, int(which)))

        ln_number = {key: i + 1 for i, key in enumerate(("OXI".index(st), t) for st, t, _ in ORDER if st in "OXI")}

        @block.tensor
        def _(pe):
            def begin(full, free, use):
                slot, n = use
                if n > 1:
                    pe.wait_ge(free[slot], n - 1)
                return slot

            def done(free, use):
                pe.wait_ge(free[use[0]], use[1])

            def project(bank, lhs, rhs, kts, stop=True):
                for kt in range(kts):
                    last = nc.tensor.matmul(bank, lhs[:, kt, :], rhs[:, kt, :], start=kt == 0, stop=stop and kt == kts - 1)
                return last

            def stage_a(t, which):
                pe.wait_ge(ld_x[t], 16)
                for j in ["kqv".index(c) for c in which]:
                    i = begin(g_full, g_free, guse["A", t, j])
                    if t == 0 and j == 0:
                        for kt in range(KT):
                            pe.wait_ge(ld_wk[kt], 16)
                            last = nc.tensor.matmul(G[i][:, :], xT_s[:, t, kt, :], wqkv_s[:, j, kt, :],
                                                    start=kt == 0, stop=kt == KT - 1)
                        last.then_inc(g_full[i], 1)
                        continue
                    if t == 0:
                        pe.wait_ge(ld_w[j], 16)
                    project(G[i][:, :], xT_s[:, t, :, :], wqkv_s[:, j, :, :], KT).then_inc(g_full[i], 1)

            def stage_b(t):
                if t == 0:
                    pe.wait_ge(ld["id"], 32)
                pe.wait_ge(s["c3_ready"], 2 * t + 2)
                for half in range(2):
                    i = begin(s_full, s_free, suse["B", t, half])
                    sc = SC[i][:, :].bitcast(bf16)
                    for c in range(H // 2):
                        last = nc.tensor.transpose(sc[0:PR, c * P:(c + 1) * P], stk[:, 0, half * (H // 2) + c, :], idb[:, :])
                    last.then_inc(s_full[i], 1)
                    for g in range(half * 2, half * 2 + 2):
                        i = begin(t_full, t_free, tuse["B", t, g])
                        tb = T[i][:, :].bitcast(bf16)
                        for c in range(HG):
                            last = nc.tensor.transpose(tb[0:PR, c * P:(c + 1) * P], stk[:, 1, g * HG + c, :], idb[:, :])
                        last.then_inc(t_full[i], 1)

            def stage_c(t, which):
                qt = t % QT
                per = HG // (1 + qt)
                if t == 0:
                    pe.wait_ge(ld["mask"], 16)
                    pe.wait_ge(ld["kaug"], 16)
                pe.wait_ge(ld_qaug[t], 16)
                for half in range(2):
                    done(s_free, suse["B", t, half])
                for g in range(NG):
                    done(t_free, tuse["B", t, g])
                for u in map(int, which):
                    i = begin(s_full, s_free, suse["C", t, u])
                    for bank in range(2):
                        cols = SC[i][:, bank * D:(bank + 1) * D].rearrange("p (h k) -> p h k", k=P * (1 + qt))
                        hb = per // 2
                        nc.tensor.matmul(cols[:, :, qt * P:(qt + 1) * P], idb[:, :],
                                         mask_s[:, 0:1, :].broadcast_to([P, hb, P]), start=True, stop=False,
                                         skip_group_check=True)
                        for c in range(hb):
                            h = u * per + bank * hb + c
                            last = nc.tensor.matmul(cols[:, c, :].rearrange("p (a k) -> p a k", k=P), qst[:, t % 2, h, :], kst[:, 0:qt + 1, h, :],
                                                    start=False, stop=c == hb - 1, skip_group_check=True)
                    last.then_inc(s_full[i], 1)

            def stage_t(t):
                pe.wait_ge(s["m4"], t + 1)
                i = begin(t_full, t_free, tuse["M", t])
                nc.tensor.transpose(T[i][:, :].bitcast(bf16)[:, 0:P], mtok[:, t, :, :].rearrange("p g c -> p (g c)"),
                                    idb[:, :]).then_inc(t_full[i], 1)

            def stage_e(t, which):
                pe.wait_ge(s["maug_ready"], t + 1)
                blks = blocks_of(t)
                for g in map(int, which):
                    for k, (kt, diagonal) in enumerate(blks):
                        i = begin(s_full, s_free, suse["E", t, g, k])
                        for bank in range(2):
                            cols = SC[i][:, bank * D:(bank + 1) * D].rearrange("p (h q) -> p h q", q=P)
                            if diagonal:
                                nc.tensor.matmul(cols[:, :, :], idb[:, :],
                                                 mask_s[:, 1:2, :].broadcast_to([P, HG // 2, P]), start=True,
                                                 stop=False, skip_group_check=True)
                            for c in range(HG // 2):
                                h = g * HG + bank * (HG // 2) + c
                                last = nc.tensor.matmul(cols[:, c, :], kst[:, kt % QT, h, :], qst[:, t % 2, h, :],
                                                        start=not diagonal, stop=(not diagonal) or c == HG // 2 - 1,
                                                        skip_group_check=True)
                        last.then_inc(s_full[i], 1)

            def stage_v(t, which):
                done(g_free, guse["A", t, 2])
                pe.wait_ge(s["const_ready"], 2)
                blks = blocks_of(t)
                for g in map(int, which):
                    if g % 2 == 0:
                        begin(t_full, t_free, tuse["E", t, g // 2])
                    i = tuse["E", t, g // 2][0]
                    for k in range(len(blks)):
                        done(s_free, suse["E", t, g, k])
                    for quad in range(2):
                        for k, (kt, _) in enumerate(blks):
                            for c in range(4):
                                col = (g % 2) * 2 + quad
                                last = nc.tensor.matmul(T[i][VW * c:VW * (c + 1), col * P:(col + 1) * P],
                                                        vaug[:, kt, g * HG + quad * 4 + c, :],
                                                        pt[:, nblk[t, g, k] % PTN, quad * 4 + c, :],
                                                        start=k == 0, stop=k == len(blks) - 1, skip_group_check=True)
                    last.then_inc(s["pv_done"] if g % 2 == 0 else t_full[i], 1)

            def stage_f(t, which):
                for half in map(int, which):
                    done(t_free, tuse["E", t, half])
                    i = begin(t_full, t_free, tuse["F", t, half])
                    for c in range(4):
                        last = nc.tensor.transpose(T[i][:, c * P:(c + 1) * P], osb[:, half, c * P:(c + 1) * P], idf[:, :])
                    last.then_inc(t_full[i], 1)

            def stage_p(t):
                for half in range(2):
                    done(t_free, tuse["F", t, half])
                i = begin(t_full, t_free, tuse["P", t])
                for c in range(KT):
                    last = nc.tensor.transpose(T[i][:, c * P:(c + 1) * P], att[:, c * P:(c + 1) * P], idf[:, :])
                last.then_inc(t_full[i], 1)

            def stage_o(t):
                if t == 0:
                    pe.wait_ge(ld["wo"], 16)
                done(t_free, tuse["P", t])
                i = begin(g_full, g_free, guse["O", t])
                project(G[i][:, :], attT, wo_s, KT).then_inc(g_full[i], 1)

            def stage_s(b):
                pe.wait_ge(s["q2_ready"], b + 1)
                pe.wait_ge(s["const_ready"], 2)
                i = begin(g_full, g_free, guse["S", b])
                for kt in range(CT):
                    last = nc.tensor.matmul(G[i][:, :], ones_b[:, :], q2_s[:, b, kt, :], start=kt == 0, stop=kt == CT - 1)
                last.then_inc(g_full[i], 1)

            def stage_g(t):
                pe.wait_ge(s["q1_ready"], t + 1)
                i = begin(t_full, t_free, tuse["G", t])
                for c in range(KT):
                    last = nc.tensor.transpose(T[i][:, :].bitcast(bf16)[:, c * P:(c + 1) * P], q1b[:, c * P:(c + 1) * P], idb[:, :])
                last.then_inc(t_full[i], 1)

            def stage_x(t):
                done(t_free, tuse["G", t])
                i = begin(g_full, g_free, guse["X", t])
                project(G[i][:, :], q1T, q2_s[:, t // QT, :, :], CT).then_inc(g_full[i], 1)

            def stage_h(t):
                pe.wait_ge(s["x2_ready"], t + 1)
                i = begin(t_full, t_free, tuse["H", t])
                for c in range(KT):
                    last = nc.tensor.transpose(T[i][:, c * P:(c + 1) * P], x2[:, t, c * P:(c + 1) * P], idf[:, :])
                last.then_inc(t_full[i], 1)

            def stage_r(t):
                if t == 0:
                    pe.wait_ge(ld["ar"], 16)
                done(t_free, tuse["H", t])
                i = begin(g_full, g_free, guse["R", t])
                project(G[i][:, 0:E + ER], x2T[:, t % 2, :, :], ar_s, KT).then_inc(g_full[i], 1)

            def stage_i(t):
                if t == 0:
                    pe.wait_ge(ld["wb"], 16)
                    pe.wait_ge(ld["lb"], 16)
                i = begin(g_full, g_free, guse["I", t])
                project(G[i][:, :], x2T[:, t % 2, :, :], wb_s, KT, stop=False)
                pe.wait_ge(s["hw_ready"], t + 1)
                j = begin(t_full, t_free, tuse["I", t])
                nc.tensor.transpose(T[j][:, 0:P], hw[:, :, :].rearrange("p e r -> p (e r)"), idf[:, :]).then_inc(t_full[j], 1)
                done(t_free, tuse["I", t])
                nc.tensor.matmul(G[i][:, :], hwT[:, :], lb_s[:, :], start=False, stop=True).then_inc(g_full[i], 1)

            stages = {"A": stage_a, "B": stage_b, "C": stage_c, "T": stage_t, "E": stage_e, "V": stage_v, "F": stage_f,
                      "P": stage_p, "O": stage_o, "S": stage_s, "G": stage_g, "X": stage_x, "H": stage_h, "R": stage_r,
                      "I": stage_i}
            for st, t, which in ORDER:
                if st in stages:
                    stages[st](t, which) if which else stages[st](t)

        @block.vector
        def _(dve):
            def full(sems, use):
                dve.wait_ge(sems[use[0]], use[1])
                return use[0]

            def tile_stats(n, src):
                nc.vector.bn_stats(stl[:, n, :], src).then_inc(s["stl_ready"], 1)
                count["stl"] += 1
                dve.wait_ge(s["stl_ready"], count["stl"])
                nc.vector.bn_aggr(mvl[:, n, :], stl[:, n, :]).then_inc(s["mvl_ready"], 1)

            def normalise(n, t, dst, src, signal):
                dve.wait_ge(s["rsl_ready"], ln_number[n, t])
                nc.vector.tensor_scalar(dst, src, mvl[:, n, 0:1], rsl[:, n, 0:1], ALU.subtract, ALU.mult).then_inc(signal, 1)

            count = {"stl": 0}
            nc.vector.memset(halfs[:, :], -0.5).then_inc(s["const_ready"], 1)

            def stage_a(t, which):
                for j in ["kqv".index(c) for c in which]:
                    i = full(g_full, guse["A", t, j])
                    if j == 2:
                        nc.vector.tensor_scalar(vaug[:, t, :, 0:DH], G[i][:, :].rearrange("p (h d) -> p h d", d=DH),
                                                -CLIP, CLIP, ALU.max, ALU.min).then_inc(g_free[i], 1)
                        continue
                    if t >= 1:
                        dve.wait_ge(s["n1_ready"], 2 * (t - 1) + j + 1)
                    nc.vector.tensor_scalar(lin[:, j, :], G[i][:, :], -CLIP, CLIP, ALU.max, ALU.min).then_inc(g_free[i], 1)
                    dve.wait_ge(g_free[i], guse["A", t, j][1])
                    nc.vector.bn_stats(st6[:, j, :], lin[:, j, :]).then_inc(s["st_ready"], 1)
                    dve.wait_ge(s["st_ready"], 2 * t + j + 1)
                    if t >= 2:
                        dve.wait_ge(s["n2_ready"], 2 * (t - 2) + j + 1)
                    nc.vector.bn_aggr(mv[:, t % 2, j, :], st6[:, j, :]).then_inc(s["mv_ready"], 1)
                if t == 0 and "v" in which:
                    dve.wait_ge(ld["scal"], 16)
                    nc.vector.reciprocal(inv_s[:, :], scal_s[:, :].rearrange("p (a c) -> p a c", c=2)[:, :, 0]).then_inc(s["inv_ready"], 1)
                    nc.vector.memset(ones_b[:, :], 1.0)
                    nc.vector.memset(vaug[:, :, :, DH:VW], 0.0).then_inc(s["vones"], 1)
                    dve.wait_ge(s["vones"], 1)
                    nc.vector.memset(vaug[:, :, :, DH:DH + 1], 1.0).then_inc(s["const_ready"], 1)

            def stage_n(t, which):
                js = ["kq".index(c) for c in which]
                sl = t % 2
                for j in js:
                    if t >= 1:
                        dve.wait_ge(s["c3_ready"], 2 * (t - 1) + j + 1)
                    dve.wait_ge(s["mv_ready"], 2 * t + j + 1)
                    if t == 0:
                        if j == 0:
                            dve.wait_ge(ld_ln["k"], 16)
                        else:
                            dve.wait_ge(s["qln_scaled"], 1)
                    nc.vector.scalar_tensor_tensor(nrm[:, j, :], lin[:, j, :], mv[:, sl, j, 0:1], ln_s[:, 2 * j, :],
                                                   ALU.subtract, ALU.mult).then_inc(s["n1_ready"], 1)
                for j in js:
                    dve.wait_ge(s["n1_ready"], 2 * t + j + 1)
                    dve.wait_ge(s["rstd_ready"], 2 * t + j + 1)
                    nc.vector.scalar_tensor_tensor(nrm[:, j, :], nrm[:, j, :], rs2[:, sl, j:j + 1], ln_s[:, 2 * j + 1, :],
                                                   ALU.mult, ALU.add).then_inc(s["n2_ready"], 1)

            def stage_d(t, which):
                for j in ["kq".index(c) for c in which]:
                    c1at, c2at, c3at = (2, 0, 1) if j == 0 else (0, 3, 4)
                    v = nrm[:, j, :].rearrange("p (h d) -> p h d", d=DH)
                    r = nrm[:, j, :].rearrange("p (h d) -> p h d", d=DH)
                    dve.wait_ge(s["c1_ready"], 2 * t + j + 1)
                    nc.vector.tensor_tensor(r, v, stk[:, j, :, c1at * DH:(c1at + 1) * DH], ALU.subtract).then_inc(s["r_ready"], 1)

            def stage_w(t, which):
                for j in ["kq".index(c) for c in which]:
                    c1at, c2at, c3at = (2, 0, 1) if j == 0 else (0, 3, 4)
                    r = nrm[:, j, :].rearrange("p (h d) -> p h d", d=DH)
                    dve.wait_ge(s["c2_ready"], 2 * t + j + 1)
                    nc.vector.tensor_tensor(stk[:, j, :, c3at * DH:(c3at + 1) * DH], r,
                                            stk[:, j, :, c2at * DH:(c2at + 1) * DH], ALU.subtract).then_inc(s["c3_ready"], 1)

            def stage_b(t):
                if t >= 2:
                    scores_done(dve, t - 2)
                for g in range(NG):
                    i = full(t_full, tuse["B", t, g])
                    nc.vector.tensor_copy(qst[0:PR, t % 2, g * HG:(g + 1) * HG, :],
                                          T[i][:, :].bitcast(bf16)[0:PR, :].rearrange("p (h q) -> p h q", q=P)).then_inc(t_free[i], 1)

            def stage_c(t, which):
                qt = t % QT
                per = HG // (1 + qt)
                for u in map(int, which):
                    i = full(s_full, suse["C", t, u])
                    nc.vector.tensor_reduce(mx[:, u * per:(u + 1) * per],
                                            SC[i][:, :].rearrange("p (h k) -> p h k", h=per), AX.X, ALU.max).then_inc(s_free[i], 1)

            def stage_m(t):
                for u in range(NG * (1 + t % QT)):
                    dve.wait_ge(s_free[suse["C", t, u][0]], suse["C", t, u][1])
                if t == 0:
                    dve.wait_ge(ld["mcols"], 16 * TILES)
                m_v = mx[:, :].rearrange("p (g c) -> p g c", c=HG)
                d_v = md[:, :].rearrange("p (g c) -> p g c", c=HG)
                nc.vector.tensor_scalar(mtok[:, t, :, 0:HG], m_v, -1.0, None, ALU.mult).then_inc(s["m1"], 1)
                dve.wait_ge(s["m1"], t + 1)
                nc.vector.scalar_tensor_tensor(d_v, m_v, -1.0, mtok[:, t, :, 0:HG], ALU.mult, ALU.subtract).then_inc(s["m2"], 1)
                dve.wait_ge(s["m2"], t + 1)
                nc.vector.tensor_copy(mtok[:, t, :, HG:2 * HG], d_v).then_inc(s["m3"], 1)
                dve.wait_ge(s["m3"], t + 1)
                nc.vector.tensor_tensor(mtok[:, t, :, 2 * HG:3 * HG], d_v, mtok[:, t, :, HG:2 * HG], ALU.subtract).then_inc(s["m4"], 1)

            def stage_u(t):
                i = full(t_full, tuse["M", t])
                nc.vector.tensor_copy(mT[:, :], T[i][:, :].bitcast(bf16)[:, 0:P]).then_inc(t_free[i], 1)
                dve.wait_ge(t_free[i], tuse["M", t][1])
                for g in range(NG):
                    last = nc.vector.tensor_copy(qst[P - AUG:P, t % 2, g * HG:(g + 1) * HG, :],
                                                 mT[AUG * g:AUG * (g + 1), :].unsqueeze(1).broadcast_to([AUG, HG, P]))
                last.then_inc(s["maug_ready"], 1)

            def stage_v(t, which):
                for half in [g // 2 for g in map(int, which) if g % 2 == 1]:
                    i = full(t_full, tuse["E", t, half])
                    if t >= 1:
                        dve.wait_ge(t_full[tuse["F", t - 1, half][0]], tuse["F", t - 1, half][1])
                    nc.vector.tensor_copy(osb[:, half, :], T[i][:, :]).then_inc(t_free[i], 1)

            def stage_f(t, which):
                for half in map(int, which):
                    i = full(t_full, tuse["F", t, half])
                    o = T[i][:, :].rearrange("p (h c) -> p h c", c=VW)
                    nc.vector.reciprocal(rsum[:, half, :], o[:, :, DH]).then_inc(s["rsum_ready"], 1)
                    dve.wait_ge(s["rsum_ready"], 2 * t + half + 1)
                    if t >= 1:
                        dve.wait_ge(t_full[tuse["P", t - 1][0]], tuse["P", t - 1][1])
                    nc.vector.tensor_tensor(att[:, half * 256:(half + 1) * 256].rearrange("p (h d) -> p h d", d=DH),
                                            o[:, :, 0:DH], rsum[:, half, :].unsqueeze(2).broadcast_to([P, H // 2, DH]),
                                            ALU.mult).then_inc(t_free[i], 1)

            def stage_o(t):
                i = full(g_full, guse["O", t])
                if t == 0:
                    dve.wait_ge(ld["xrow"], 16)
                if t >= 1:
                    dve.wait_ge(s["q1_ready"], t)
                nc.vector.tensor_tensor(r1[:, :], G[i][:, :], x_s[:, t, :], ALU.add).then_inc(g_free[i], 1)
                dve.wait_ge(g_free[i], guse["O", t][1])
                tile_stats(0, r1[:, :])

            def stage_q(t):
                normalise(0, t, x1[:, t, :], r1[:, :], s["x1_ready"])
                dve.wait_ge(s["x1_ready"], t + 1)
                nc.vector.tensor_scalar(qd[:, :], x1[:, t, :], inv_s[:, 0:1], scal_s[:, 1:2], ALU.mult, ALU.add).then_inc(s["qd1"], 1)
                dve.wait_ge(s["qd1"], t + 1)
                nc.vector.tensor_scalar(qd[:, :], qd[:, :], QMAX, ROUND, ALU.min, ALU.add).then_inc(s["qd2"], 1)
                dve.wait_ge(s["qd2"], t + 1)
                if t >= 1:
                    dve.wait_ge(s["rowsum_ready"], t)
                    dve.wait_ge(t_full[tuse["G", t - 1][0]], tuse["G", t - 1][1])
                nc.vector.tensor_scalar(q1b[:, :], qd[:, :], ROUND, -(ROUND + CENTRE), ALU.max, ALU.add).then_inc(s["q1_ready"], 1)

            def stage_s(b):
                if b == 0:
                    z = scal_s[:, :].rearrange("p (a c) -> p a c", c=2)
                    nc.vector.tensor_scalar(a12[:, :], z[:, :, 1], -1.0, CENTRE, ALU.mult, ALU.add).then_inc(s["sc1"], 1)
                    nc.vector.tensor_tensor(s12[:, :], scal_s[:, 0:1], scal_s[:, 2:3], ALU.mult).then_inc(s["sc1"], 1)
                    dve.wait_ge(s["sc1"], 2)
                    nc.vector.tensor_scalar(kaa[:, :], a12[:, 0:1], a12[:, 1:2], float(CTX), ALU.mult, ALU.mult).then_inc(s["sc2"], 1)
                    dve.wait_ge(s["sc2"], 1)
                i = full(g_full, guse["S", b])
                nc.vector.tensor_scalar(colc[:, b, :], G[i][:, :], a12[:, 0:1], kaa[:, :], ALU.mult, ALU.add).then_inc(g_free[i], 1)

            def stage_z(b):
                dve.wait_ge(s["q2a"], b + 1)
                nc.vector.tensor_scalar(ctx_s[:, :, :], ctx_s[:, :, :], QMAX, ROUND, ALU.min, ALU.add).then_inc(s["q2b"], 1)
                dve.wait_ge(s["q2b"], b + 1)
                nc.vector.tensor_scalar(q2_s[:, b, :, :], ctx_s[:, :, :], ROUND, -(ROUND + CENTRE), ALU.max,
                                        ALU.add).then_inc(s["q2_ready"], 1)

            def stage_x(t):
                b = t // QT
                dve.wait_ge(s["rowsum_ready"], t + 1)
                nc.vector.tensor_tensor(arq[:, :], rsq[:, :], a12[:, 1:2], ALU.mult).then_inc(s["arq_ready"], 1)
                dve.wait_ge(s["arq_ready"], t + 1)
                i = full(g_full, guse["X", t])
                dve.wait_ge(g_free[guse["S", b][0]], guse["S", b][1])
                if t >= 1:
                    dve.wait_ge(s["x2_ready"], t)
                nc.vector.scalar_tensor_tensor(r2[:, :], G[i][:, :], arq[:, :], colc[:, b, :], ALU.add, ALU.add).then_inc(g_free[i], 1)
                dve.wait_ge(g_free[i], guse["X", t][1])
                nc.vector.scalar_tensor_tensor(r2[:, :], r2[:, :], s12[:, :], x1[:, t, :], ALU.mult, ALU.add).then_inc(s["r2_ready"], 1)
                dve.wait_ge(s["r2_ready"], t + 1)
                tile_stats(1, r2[:, :])

            def stage_y(t):
                normalise(1, t, x2[:, t, :], r2[:, :], s["x2_ready"])

            def stage_r(t):
                i = full(g_full, guse["R", t])
                sl = t % 2
                nc.vector.tensor_copy(lg[:, sl, :], G[i][:, 0:E + ER]).then_inc(g_free[i], 1)
                dve.wait_ge(g_free[i], guse["R", t][1])
                nc.vector.max(top[:, :], lg[:, sl, 0:E]).then_inc(s["top_ready"], 1)
                dve.wait_ge(s["top_ready"], t + 1)
                if t >= 1:
                    dve.wait_ge(s["ex_ready"], t)
                nc.vector.tensor_tensor(dl[:, :], top[:, 1:2], top[:, 0:1], ALU.subtract).then_inc(s["dl_ready"], 1)
                nc.vector.max_index(idx[:, :], top[:, :], lg[:, sl, 0:E]).then_inc(s["idx_ready"], 1)
                dve.wait_ge(s["idx_ready"], t + 1)
                nc.vector.tensor_copy(idxf[:, :], idx[:, 0:2]).then_inc(s["idxf_ready"], 1)
                dve.wait_ge(s["ex_ready"], t + 1)
                nc.vector.tensor_scalar(den[:, :], ex[:, :], 1.0, 1.0 / LORA_SCALE, ALU.add, ALU.mult).then_inc(s["den_ready"], 1)
                dve.wait_ge(s["den_ready"], t + 1)
                nc.vector.reciprocal(w01[:, 0:1], den[:, :]).then_inc(s["w0_ready"], 1)
                dve.wait_ge(s["w0_ready"], t + 1)
                nc.vector.tensor_tensor(w01[:, 1:2], w01[:, 0:1], ex[:, :], ALU.mult).then_inc(s["w1_ready"], 1)
                dve.wait_ge(s["w1_ready"], t + 1)
                dve.wait_ge(s["idxf_ready"], t + 1)
                for j in range(2):
                    nc.vector.tensor_scalar(wsel[:, j, :], iota_s[:, :], idxf[:, j:j + 1], w01[:, j:j + 1],
                                            ALU.is_equal, ALU.mult).then_inc(s["ws0"], 1)
                dve.wait_ge(s["ws0"], 2 * t + 2)
                nc.vector.tensor_tensor(wsel[:, 0, :], wsel[:, 0, :], wsel[:, 1, :], ALU.add).then_inc(s["wsel_ready"], 1)
                dve.wait_ge(s["wsel_ready"], t + 1)
                if t >= 1:
                    dve.wait_ge(t_full[tuse["I", t - 1][0]], tuse["I", t - 1][1])
                nc.vector.tensor_tensor(hw[:, :, :], lg[:, sl, E:E + ER].rearrange("p (e r) -> p e r", r=R),
                                        wsel[:, 0, :].unsqueeze(2).broadcast_to([P, E, R]), ALU.mult).then_inc(s["hw_ready"], 1)

            def stage_i(t):
                i = full(g_full, guse["I", t])
                dve.wait_ge(s["xb_ready"], t + 1)
                if t >= 1:
                    dve.wait_ge(s["x3_ready"], t)
                nc.vector.tensor_tensor(r3[:, :], G[i][:, :], xb[:, t % 2, :], ALU.add).then_inc(g_free[i], 1)
                dve.wait_ge(g_free[i], guse["I", t][1])
                tile_stats(2, r3[:, :])

            def stage_j(t):
                normalise(2, t, x3[:, t, :], r3[:, :], s["x3_ready"])

            stages = {"A": stage_a, "N": stage_n, "B": stage_b, "C": stage_c, "M": stage_m, "U": stage_u, "D": stage_d, "W": stage_w, "V": stage_v, "F": stage_f,
                      "O": stage_o, "S": stage_s, "X": stage_x, "R": stage_r, "I": stage_i, "Z": stage_z,
                      "Q": stage_q, "Y": stage_y, "J": stage_j}
            for st, t, which in ORDER:
                if st in stages:
                    stages[st](t, which) if which else stages[st](t)

        @block.scalar
        def _(act):
            def values_done(m):
                t, g = m
                if g % 2 == 0:
                    act.wait_ge(s["pv_done"], NG // 2 * t + g // 2 + 1)
                else:
                    full(t_full, tuse["E", t, g // 2])

            def full(sems, use):
                act.wait_ge(sems[use[0]], use[1])
                return use[0]

            def stage_l(_):
                act.wait_ge(ld_ln["q"], 16)
                nc.scalar.activation(ln_s[:, 2:4, :], ln_s[:, 2:4, :], ACT.Copy, scale=DH ** -0.5).then_inc(s["qln_scaled"], 1)

            def stage_z(b):
                act.wait_ge(ld["ctx"], 16 * (b + 1))
                act.wait_ge(s["inv_ready"], 1)
                nc.scalar.activation(ctx_s[:, :, :], ctx_s[:, :, :], ACT.Identity, bias=scal_s[:, 3:4],
                                     scale=inv_s[:, 1:2]).then_inc(s["q2a"], 1)

            def stage_n(t, which):
                js = ["kq".index(c) for c in which]
                for j in js:
                    act.wait_ge(s["n2_ready"], 2 * t + j + 1)
                    if t >= 1:
                        for n in range(2):
                            if j == 0:
                                full(s_full, suse["B", t - 1, n])
                            else:
                                full(t_full, tuse["B", t - 1, NG - 1 - n])
                    at = 2 if j == 0 else 0
                    nc.scalar.activation(
                        stk[:, j, :, at * DH:(at + 3) * DH].rearrange("p h (a d) -> p h a d", d=DH),
                        nrm[:, j, :].rearrange("p (h d) -> p h d", d=DH).unsqueeze(2).broadcast_to([P, H, 3, DH]),
                        ACT.Copy).then_inc(s["c1_ready"], 1)

            def stage_d(t, which):
                for j in ["kq".index(c) for c in which]:
                    act.wait_ge(s["r_ready"], 2 * t + j + 1)
                    at, step = (0, 5) if j == 0 else (3, 2)
                    parts = stk[:, j, :, :].rearrange("p h (a d) -> p h a d", d=DH)
                    nc.scalar.activation(
                        parts[:, :, at:at + step + 1:step, :],
                        nrm[:, j, :].rearrange("p (h d) -> p h d", d=DH).unsqueeze(2).broadcast_to([P, H, 2, DH]),
                        ACT.Copy).then_inc(s["c2_ready"], 1)

            def stage_b(t):
                if t >= QT:
                    scores_done(act, t - t % QT - 1)
                for half in range(2):
                    i = full(s_full, suse["B", t, half])
                    nc.scalar.activation(kst[0:PR, t % QT, half * (H // 2):(half + 1) * (H // 2), :],
                                         SC[i][:, :].bitcast(bf16)[0:PR, :].rearrange("p (h q) -> p h q", q=P),
                                         ACT.Copy).then_inc(s_free[i], 1)

            def stage_e(t, which):
                for g in map(int, which):
                    for k in range(len(blocks_of(t))):
                        i = full(s_full, suse["E", t, g, k])
                        n = nblk[t, g, k]
                        if n >= PTN:
                            values_done(grp_of[n - PTN])
                        nc.scalar.activation(pt[:, n % PTN, :, :].rearrange("p h q -> p (h q)"), SC[i][:, :], ACT.Exp).then_inc(s_free[i], 1)

            def stage_p(t):
                i = full(t_full, tuse["P", t])
                if t >= 1:
                    use = guse["O", t - 1]
                    act.wait_ge(g_full[use[0]], use[1])
                nc.scalar.activation(attT[:, :, :].rearrange("p a b -> p (a b)"), T[i][:, :], ACT.Copy).then_inc(t_free[i], 1)

            def stage_g(t):
                i = full(t_full, tuse["G", t])
                if t >= 1:
                    use = guse["X", t - 1]
                    act.wait_ge(g_full[use[0]], use[1])
                nc.scalar.activation(q1T[:, :, :].rearrange("p a b -> p (a b)"), T[i][:, :].bitcast(bf16)[:, 0:D], ACT.Copy).then_inc(t_free[i], 1)
                if t >= 1:
                    act.wait_ge(s["arq_ready"], t)
                nc.scalar.activation(junk[:, :], q1b[:, :], ACT.Copy, accum_out=rsq[:, :]).then_inc(s["rowsum_ready"], 1)

            def stage_h(t):
                i = full(t_full, tuse["H", t])
                nc.scalar.activation(x2T[:, t % 2, :, :].rearrange("p a b -> p (a b)"), T[i][:, :], ACT.Copy).then_inc(t_free[i], 1)

            def stage_r(t):
                act.wait_ge(s["dl_ready"], t + 1)
                if t >= 1:
                    act.wait_ge(s["w1_ready"], t)
                nc.scalar.activation(ex[:, :], dl[:, :], ACT.Exp).then_inc(s["ex_ready"], 1)

            def stage_i(t):
                i = full(t_full, tuse["I", t])
                if t >= 1:
                    use = guse["I", t - 1]
                    act.wait_ge(g_full[use[0]], use[1])
                nc.scalar.activation(hwT[:, :], T[i][:, 0:P], ACT.Copy).then_inc(t_free[i], 1)

            stages = {"L": stage_l, "N": stage_n, "D": stage_d, "B": stage_b, "E": stage_e, "P": stage_p, "G": stage_g,
                      "H": stage_h, "R": stage_r, "I": stage_i, "Z": stage_z}
            for st, t, which in ORDER:
                if st in stages:
                    stages[st](t, which) if which else stages[st](t)

        @block.gpsimd
        def _(pool):
            def rstd(dst, tmp, var, n, ready, mid):
                nc.gpsimd.tensor_scalar(tmp, var, EPS, None, ALU.add).then_inc(s[mid], 1)
                count[mid] += 1
                pool.wait_ge(s[mid], count[mid])
                nc.gpsimd.tensor_tensor(dst, tmp, halfs[:, 0:n], ALU.pow).then_inc(s[ready], 1)
                count[ready] += 1

            count = {"ve_ready": 0, "rstd_ready": 0, "vel_ready": 0, "rsl_ready": 0}

            def stage_a(t, which):
                sl = t % 2
                if t == 0 and "k" in which:
                    pool.wait_ge(s["const_ready"], 1)
                for j in ["kqv".index(c) for c in which if c != "v"]:
                    pool.wait_ge(s["mv_ready"], 2 * t + j + 1)
                    rstd(rs2[:, sl, j:j + 1], ve2[:, j:j + 1], mv[:, sl, j, 1:2], 1, "rstd_ready", "ve_ready")

            def stage_o(t):
                ln_rstd(0)

            def ln_rstd(n):
                count["mvl"] = count.get("mvl", 0) + 1
                pool.wait_ge(s["mvl_ready"], count["mvl"])
                rstd(rsl[:, n, :], vel[:, n, :], mvl[:, n, 1:2], 1, "rsl_ready", "vel_ready")

            def stage_x(t):
                ln_rstd(1)

            def stage_y(t):
                pool.wait_ge(s["x2_ready"], t + 1)
                if t == 0:
                    pool.wait_ge(ld_ln["base"], 16)
                if t >= 2:
                    pool.wait_ge(g_free[guse["I", t - 2][0]], guse["I", t - 2][1])
                nc.gpsimd.tensor_tensor(xb[:, t % 2, :], x2[:, t, :], ln_s[:, 4, :], ALU.add).then_inc(s["xb_ready"], 1)
                count["xb_ready"] = t + 1

            def stage_i(t):
                ln_rstd(2)

            stages = {"A": stage_a, "O": stage_o, "X": stage_x, "Y": stage_y, "I": stage_i}
            for st, t, which in ORDER:
                if st in stages:
                    stages[st](t, which) if which else stages[st](t)


def three_parts(a):
    bfloat16 = mybir.dt.np(mybir.dt.bfloat16)
    a = a.astype(np.float64)
    hi = a.astype(np.float32).astype(bfloat16)
    mid = (a - hi.astype(np.float64)).astype(np.float32).astype(bfloat16)
    lo = (a - hi.astype(np.float64) - mid.astype(np.float64)).astype(np.float32).astype(bfloat16)
    return hi, mid, lo


def constants():
    bfloat16 = mybir.dt.np(mybir.dt.bfloat16)
    ident = np.eye(P, dtype=np.float32)
    i = np.arange(P)
    mask = np.where(i[:, None] >= i[None, :], 0.0, MASKED).astype(np.float32)
    masks = np.stack([mask, mask.T], axis=1).astype(bfloat16)
    slopes = (1.0 / np.power(np.float32(2.0), np.arange(1, H + 1, dtype=np.float32) * np.float32(8.0 / H))).astype(np.float32)
    pos = np.arange(S)
    kaug = np.zeros((AUG, QT, H, P), dtype=bfloat16)
    rise = three_parts(slopes[:, None].astype(np.float64) * pos[None, :])
    fall = three_parts(-slopes)
    for h in range(H):
        for part in range(3):
            kaug[part * HG + h % HG, :, h, :] = 1.0
            kaug[3 * HG + part, :, h, :] = rise[part][h].reshape(QT, P)
            kaug[3 * HG + 3 + part, :, h, :] = fall[part][h]
    qaug = np.zeros((AUG, QT, P), dtype=bfloat16)
    qaug[3 * HG:3 * HG + 3] = 1.0
    qaug[3 * HG + 3:3 * HG + 6] = pos.reshape(QT, P)[None]
    mcols = np.zeros((QT, P, H // HG, AUG), dtype=bfloat16)
    mcols[:] = np.transpose(qaug, (1, 2, 0))[:, :, None, :]
    iota = np.broadcast_to(np.arange(E, dtype=np.float32), (P, E)).copy()
    qaug = np.ascontiguousarray(np.broadcast_to(qaug.transpose(1, 0, 2)[:, :, None, :], (QT, AUG, H, P)))
    return ident, ident.astype(bfloat16), masks, kaug, qaug, mcols, iota


def kernel(**inputs):
    import concourse.bacc as _bacc
    from concourse.bass_utils import run_bass_kernel_spmd as _run

    f = {k: np.asarray(v) for k, v in inputs.items()}

    def rows(w, n):
        return np.ascontiguousarray(w.reshape(-1, P, n).transpose(1, 0, 2))

    x = f["x"].reshape(B * S, D)
    xT = np.ascontiguousarray(x.reshape(TILES, P, KT, P).transpose(0, 3, 2, 1))
    xrow = np.ascontiguousarray(x.reshape(TILES, P, D).transpose(1, 0, 2))
    wq, wk, wv = f["L0_attn_w_qkv"].reshape(3, D, D)
    wqkvT = np.stack([rows(w.T, D) for w in (wk, wq, wv)])
    ln = np.stack([f["L0_attn_k_ln_w"], f["L0_attn_k_ln_b"], f["L0_attn_q_ln_w"], f["L0_attn_q_ln_b"], f["L0_ffn_b_base"]])
    ln = ln[None]
    woT = rows(f["L0_attn_w_out"].T, D)
    ctx4 = np.stack([rows(f["ctx_4096"][b], D) for b in range(B)])
    scal = np.concatenate([f["L0_xattn_x1_scale"], f["L0_xattn_x1_zp"], f["L0_xattn_x2_scale"], f["L0_xattn_x2_zp"]])
    scal = np.ascontiguousarray(np.broadcast_to(scal, (P, 4)))
    wbT = rows(f["L0_ffn_W_base"].T, D)
    arT = rows(np.concatenate([f["L0_ffn_W_router"], f["L0_ffn_A"].reshape(ER, D)]).T, E + ER)
    loraB = np.ascontiguousarray(f["L0_ffn_B"].transpose(0, 2, 1).reshape(ER, D))
    ident, identb, masks, kaug, qaug, mcols, iota = constants()

    nc = _bacc.Bacc("TRN2", target_bir_lowering=False, num_devices=1)
    arrays, args = {}, []
    for name, a in dict(xT=xT, xrow=xrow, wqkvT=wqkvT, ln=ln, woT=woT, ctx4=ctx4, scal=scal, wbT=wbT, arT=arT, loraB=loraB,
                        identf=ident, identb=identb, maskc=masks, kaug=kaug, qaug=qaug, mcols=mcols, iota=iota).items():
        a = np.ascontiguousarray(a)
        arrays[name + "_dram"] = a
        args.append(nc.dram_tensor(name + "_dram", a.shape, mybir.dt.from_np(a.dtype), kind="ExternalInput").ap())
    out = nc.dram_tensor("out_dram", (TILES, P, D), mybir.dt.float32, kind="ExternalOutput").ap()
    build(nc, *args, out)
    r = _run(nc, [arrays], core_ids=[0])
    return r.results[0]["out_dram"].reshape(B, S, D)
```

```python
import numpy as np
import concourse.bass as bass
from concourse import mybir
from contextlib import ExitStack

P = 128
B, S, D = 2, 256, 512
TILES = B * S // P
QT = S // P
KT = D // P
H = 32
DH = D // H
PARTS = 6
PR = PARTS * DH
AUG = 32
HG = 8
NG = H // HG
VW = 32
PTN = 4
E = 8
R = 16
ER = E * R
FIRST = [(2, 3, 4), (0, 1, 2)]
SECOND = [(0, 5), (3, 5)]
THIRD = [1, 4]
CTX = 512
CT = CTX // P
WARM_UP = 8
CLIP = 8.0
EPS = 1e-5
LORA_SCALE = 2.0
MASKED = -1e30
QMAX = 255.0
CENTRE = 128.0
ROUND = 1.5 * 2.0 ** 23

ORDER = [(w[0], int(w[1]), w[2:]) for w in """
    A0k L0 N0k A0q D0k N0q A1k D0q W0k W0q A0v A1q B00 B01 N1k N1q C001 D1k A1v W1k D1q C02 C03 M0 W1q A2k A2v
    T0 U0 B10 E00 A2q E01 B11 E02 V00 E03 V01 N2k C10 V02 N2q C11 F00 V03 C12 D2k D2q A3v C13 C14 F01 A3k W2k
    C156 P0 A3q C17 W2q M1 O0 T1 U1 Z0 B20 Q0 E10 B21 S0 E11 G0 C20 C21 V10 E12 N3k N3q C22 C23 V11 E13 M2 V12
    T2 D3k W3k V13 U2 E20 D3q F10 F11 X0 E21 Y0 P1 W3q Z1 E22 V20 O1 V21 B30 Q1 E23 V22 C301 V23 H0 F20 C32 B31
    C33 F21 C34 C35 P2 R0 G1 C367 M3 O2 T3 U3 K0 E30 w0 X1 E31 Y1 Q2 V30 I0 V31 E32 H1 F30 E33 V32 G2 V33 S1 F31
    X2 P3 R1 Y2 J0 O3 w1 H2 Q3 K1 I1 G3 R2 w2 X3 J1 K2 Y3 I2 H3 R3 K3 w3 J2 I3 J3
    """.split()]


def bank_uses(keys, slots):
    return {key: (i % slots, i // slots + 1) for i, key in enumerate(keys)}


def blocks_of(t):
    return [(k, k == t) for k in range(t - t % QT, t + 1)]


def build(nc, xT, xrow, wqkvT, ln, woT, ctx4, scal, wbT, arT, loraB, identf, identb, maskc, kaug, qaug, mcols, iota, out):
    fp32, bf16, u32 = mybir.dt.float32, mybir.dt.bfloat16, mybir.dt.uint32
    ALU = mybir.AluOpType
    ACT = mybir.ActivationFunctionType
    AX = mybir.AxisListType

    ctx = ExitStack()
    with ctx:
        def sb(name, shape, dt=fp32):
            return ctx.enter_context(nc.sbuf_tensor(name, shape, dt))

        def pb(name, shape, dt=fp32):
            return ctx.enter_context(nc.psum_tensor(name, shape, dt))

        def sem(name):
            return ctx.enter_context(nc.semaphore(name))

        xT_s = sb("xT_s", [P, TILES, KT, P])
        x_s = sb("x_s", [P, TILES, D])
        wqkv_s = sb("wqkv_s", [P, 3, KT, D])
        ln_s = sb("ln_s", [P, 5, D])
        wo_s = sb("wo_s", [P, KT, D])
        ctx_s = xT_s[:, :, :, :].rearrange("p t k c -> p (t k c)").rearrange("p (c d) -> p c d", d=D)
        q2_s = sb("q2_s", [P, 2, CT, D], bf16)
        wb_s = wqkv_s[:, 0, :, :]
        ar_s = sb("ar_s", [P, KT, E + ER])
        lb_s = sb("lb_s", [ER, D])
        idf = sb("idf", [P, P])
        idb = sb("idb", [P, P], bf16)
        mask_s = sb("mask_s", [P, 2, P], bf16)
        ones_b = sb("ones_b", [P, P], bf16)
        iota_s = sb("iota_s", [P, E])
        scal_s = sb("scal_s", [P, 4])
        a12 = sb("a12", [P, 2])
        inv_s = sb("inv_s", [P, 2])
        s12 = sb("s12", [P, 1])
        kaa = sb("kaa", [P, 1])
        halfs = sb("halfs", [P, 2])
        kst = sb("kst", [P, TILES, H, P], bf16)
        qst = sb("qst", [P, 2, H, P], bf16)
        vaug = sb("vaug", [P, TILES, H, VW])
        lin = sb("lin", [P, 2, D])
        nrm = sb("nrm", [P, 2, D])
        stk = sb("stk", [P, 2, H, PR], bf16)
        st6 = sb("st6", [P, 2, 6])
        mv = sb("mv", [P, 2, 2, 2])
        rs2 = sb("rs2", [P, 2, 2])
        ve2 = sb("ve2", [P, 2])
        mx = sb("mx", [P, H])
        md = sb("md", [P, H])
        mtok = sb("mtok", [P, TILES, NG, AUG], bf16)
        mT = sb("mT", [P, P], bf16)
        pt = sb("pt", [P, PTN, HG, P])
        osb = sb("osb", [P, 2, D])
        rsum = sb("rsum", [P, 2, H // 2])
        att = sb("att", [P, D])
        attT = sb("attT", [P, KT, P])
        r1, r2, r3 = [sb(f"r{n}", [P, D]) for n in (1, 2, 3)]
        qd = r1
        x1 = x2 = x3 = x_s
        stl = sb("stl", [P, 3, 6])
        mvl = sb("mvl", [P, 3, 2])
        vel = sb("vel", [P, 3, 1])
        rsl = sb("rsl", [P, 3, 1])
        q1b = sb("q1b", [P, D], bf16)
        unread = sb("unread", [P, D], bf16)
        rsq = sb("rsq", [P, 1])
        arq = sb("arq", [P, 1])
        q1T = sb("q1T", [P, KT, P], bf16)
        colc = sb("colc", [P, 2, D])
        xb = sb("xb", [P, 2, D])
        x2T = sb("x2T", [P, 2, KT, P])
        lg = sb("lg", [P, 2, E + ER])
        top = sb("top", [P, 8])
        idx = sb("idx", [P, 8], u32)
        idxf = sb("idxf", [P, 2])
        dl = sb("dl", [P, 1])
        ex = sb("ex", [P, 1])
        den = sb("den", [P, 1])
        w01 = sb("w01", [P, 2])
        wsel = sb("wsel", [P, 2, E])
        hw = sb("hw", [P, E, R])
        hwT = sb("hwT", [P, P])

        G = [pb(f"G{i}", [P, D]) for i in range(2)]
        T = [pb(f"T{i}", [P, D]) for i in range(2)]
        SC = [pb(f"SC{i}", [P, 2 * D]) for i in range(2)]
        gkeys, tkeys, skeys = [], [], []
        for st, t, which in ORDER:
            if st == "A":
                gkeys += [("A", t, "kqv".index(c)) for c in which]
            if st == "B":
                for half in map(int, which):
                    skeys += [("B", t, half)]
                    tkeys += [("B", t, g) for g in range(2 * half, 2 * half + 2)]
            if st == "C":
                skeys += [("C", t, int(g)) for g in which]
            if st == "E":
                skeys += [("E", t, int(which), k) for k in range(len(blocks_of(t)))]
            if st == "V" and which in "02":
                tkeys += [("E", t, int(which) // 2)]
            if st == "F":
                tkeys += [("F", t, int(which))]
            if st == "T":
                tkeys += [("M", t)]
            if st in "PGHI":
                tkeys += [(st, t)]
            if st == "K":
                gkeys += [("I", t)]
            if st in "OSXR":
                gkeys += [(st, t)]
        guse, tuse, suse = bank_uses(gkeys, 2), bank_uses(tkeys, 2), bank_uses(skeys, 2)
        g_full, g_free = [sem(f"g_full{i}") for i in range(2)], [sem(f"g_free{i}") for i in range(2)]
        t_full, t_free = [sem(f"t_full{i}") for i in range(2)], [sem(f"t_free{i}") for i in range(2)]
        s_full, s_free = [sem(f"s_full{i}") for i in range(2)], [sem(f"s_free{i}") for i in range(2)]

        ld_x = [sem(f"ld_x{t}") for t in range(TILES)]
        ld_qaug = [sem(f"ld_qaug{t}") for t in range(TILES)]
        ld_ln = {what: sem("ld_ln_" + what) for what in ("k", "q", "base")}
        ld_wk = [sem(f"ld_wk{kt}") for kt in range(KT)]
        ld_w = [sem(f"ld_w{j}") for j in range(3)]
        names = "id mask kaug mcols xrow wo ctx scal wb ar lb iota".split()
        ld = {n: sem("ld_" + n) for n in names}

        prod = (
            "ones_ready const_ready vones inv_ready qln_scaled sc1 sc2 "
            "st_ready mv_ready ve_ready rstd_ready n1_ready n2_ready c1_ready r_ready c2_ready c3_ready "
            "m1 m2 m3 m4 maug_ready "
            "pv_done rsum_ready "
            "stl_ready mvl_ready vel_ready rsl_ready "
            "x1_ready qd1 qd2 q1_ready rowsum_ready arq_ready q2a q2b q2_ready "
            "r2_ready x2_ready xb_ready top_ready dl_ready idx_ready idxf_ready ex_ready den_ready w0_ready "
            "w1_ready ws0 wsel_ready hw_ready x3_ready out_done").split()
        s = {n: sem(n) for n in prod}

        def scores_done(eng, t):
            for g in range(NG - 2, NG):
                for k in range(len(blocks_of(t))):
                    eng.wait_ge(s_full[suse["E", t, g, k][0]], suse["E", t, g, k][1])

        block = ctx.enter_context(nc.Block())

        @block.sync
        def _(sp):
            def load(dst, src, signal):
                sp.dma_start(dst, src).then_inc(signal, 16)

            def load_ln(what, first, count):
                load(ln_s[:, first:first + count, :], ln[:, first:first + count, :].broadcast_to([P, count, D]), ld_ln[what])

            load(xT_s[:, 0, :, :], xT[0], ld_x[0])
            for kt in range(KT):
                load(wqkv_s[:, 0, kt, :], wqkvT[0, :, kt, :], ld_wk[kt])
            load(wqkv_s[:, 1, :, :], wqkvT[1], ld_w[1])
            load_ln("k", 0, 2)
            load_ln("q", 2, 2)
            load(xT_s[:, 1, :, :], xT[1], ld_x[1])
            load(wqkv_s[:, 2, :, :], wqkvT[2], ld_w[2])
            load(scal_s[:, :], scal, ld["scal"])
            load(idf[:, :], identf, ld["id"])
            load(idb[:, :], identb, ld["id"])
            load(mask_s[:, :, :], maskc, ld["mask"])
            for t in range(2):
                load(qst[P - AUG:P, t, :, :], qaug[t % QT], ld_qaug[t])
            for b in range(B):
                load(kst[P - AUG:P, b * QT:(b + 1) * QT, :, :], kaug, ld["kaug"])
            for t in range(TILES):
                load(mtok[:, t, :, :], mcols[t % QT], ld["mcols"])
            for t in range(2, TILES):
                load(xT_s[:, t, :, :], xT[t], ld_x[t])
            load(iota_s[:, :], iota, ld["iota"])
            load(x_s[:, :, :], xrow, ld["xrow"])
            load(wo_s[:, :, :], woT, ld["wo"])
            load(ar_s[:, :, :], arT, ld["ar"])
            load_ln("base", 4, 1)
            load(lb_s[:, :], loraB, ld["lb"])
            projected = set()
            for st, t, which in ORDER:
                if st == "A" and t == TILES - 1:
                    projected |= set(which)
                    for c in which:
                        slot, n = guse["A", t, "kqv".index(c)]
                        sp.wait_ge(g_full[slot], n)
                    if "k" in which:
                        load(wb_s, wbT, ld["wb"])
                    if len(projected) == 3:
                        load(ctx_s[:, :, :], ctx4[0], ld["ctx"])
                if st == "Z" and t + 1 < B:
                    sp.wait_ge(s["q2_ready"], t + 1)
                    load(ctx_s[:, :, :], ctx4[t + 1], ld["ctx"])
                if st == "E" and str(NG - 1) in which and t + 2 < TILES:
                    scores_done(sp, t)
                    load(qst[P - AUG:P, t % 2, :, :], qaug[(t + 2) % QT], ld_qaug[t + 2])
                if st == "J":
                    sp.wait_ge(s["x3_ready"], t + 1)
                    sp.dma_start(out[t], x3[:, t, :]).then_inc(s["out_done"], 16)
            sp.wait_ge(s["out_done"], 16 * TILES)

        nblk, grp_of = {}, []
        for st, t, which in ORDER:
            if st == "E":
                for k in range(len(blocks_of(t))):
                    nblk[t, int(which), k] = len(grp_of)
                    grp_of.append((t, int(which)))

        ln_number = {key: i + 1 for i, key in enumerate(("OXI".index(st), t) for st, t, _ in ORDER if st in "OXI")}

        @block.tensor
        def _(pe):
            def begin(full, free, use):
                slot, n = use
                if n > 1:
                    pe.wait_ge(free[slot], n - 1)
                return slot

            def done(free, use):
                pe.wait_ge(free[use[0]], use[1])

            def project(bank, lhs, rhs, kts, stop=True):
                for kt in range(kts):
                    last = nc.tensor.matmul(bank, lhs[:, kt, :], rhs[:, kt, :], start=kt == 0, stop=stop and kt == kts - 1)
                return last

            pe.wait_ge(s["ones_ready"], 1)
            for _ in range(WARM_UP):
                nc.tensor.matmul(SC[0][:, 0:D].rearrange("p (a k) -> p a k", k=P), ones_b[:, :],
                                 ones_b[:, :].unsqueeze(1).broadcast_to([P, D // P, P]), start=True, stop=True)

            def stage_a(t, which):
                pe.wait_ge(ld_x[t], 16)
                for j in ["kqv".index(c) for c in which]:
                    i = begin(g_full, g_free, guse["A", t, j])
                    if t == 0 and j == 0:
                        for kt in range(KT):
                            pe.wait_ge(ld_wk[kt], 16)
                            last = nc.tensor.matmul(G[i][:, :], xT_s[:, t, kt, :], wqkv_s[:, j, kt, :],
                                                    start=kt == 0, stop=kt == KT - 1)
                        last.then_inc(g_full[i], 1)
                        continue
                    if t == 0:
                        pe.wait_ge(ld_w[j], 16)
                    project(G[i][:, :], xT_s[:, t, :, :], wqkv_s[:, j, :, :], KT).then_inc(g_full[i], 1)

            def stage_b(t, which):
                if t == 0:
                    pe.wait_ge(ld["id"], 32)
                pe.wait_ge(s["c3_ready"], 2 * t + 2)
                for half in map(int, which):
                    i = begin(s_full, s_free, suse["B", t, half])
                    sc = SC[i][:, :].bitcast(bf16)
                    for c in range(H // 2):
                        last = nc.tensor.transpose(sc[0:PR, c * P:(c + 1) * P], stk[:, 0, half * (H // 2) + c, :], idb[:, :])
                    last.then_inc(s_full[i], 1)
                    for g in range(half * 2, half * 2 + 2):
                        i = begin(t_full, t_free, tuse["B", t, g])
                        tb = T[i][:, :].bitcast(bf16)
                        for c in range(HG):
                            last = nc.tensor.transpose(tb[0:PR, c * P:(c + 1) * P], stk[:, 1, g * HG + c, :], idb[:, :])
                        last.then_inc(t_full[i], 1)

            def stage_c(t, which):
                qt = t % QT
                per = HG // (1 + qt)
                if t == 0:
                    pe.wait_ge(ld["mask"], 16)
                    pe.wait_ge(ld["kaug"], 16 * B)
                pe.wait_ge(ld_qaug[t], 16)
                for u in map(int, which):
                    half = u * per // (H // 2)
                    done(s_free, suse["B", t, half])
                    for g in range(2 * half, 2 * half + 2):
                        done(t_free, tuse["B", t, g])
                    i = begin(s_full, s_free, suse["C", t, u])
                    for bank in range(2):
                        cols = SC[i][:, bank * D:(bank + 1) * D].rearrange("p (h k) -> p h k", k=P * (1 + qt))
                        hb = per // 2
                        nc.tensor.matmul(cols[:, :, qt * P:(qt + 1) * P], idb[:, :],
                                         mask_s[:, 0:1, :].broadcast_to([P, hb, P]), start=True, stop=False,
                                         skip_group_check=True)
                        for c in range(hb):
                            h = u * per + bank * hb + c
                            last = nc.tensor.matmul(cols[:, c, :].rearrange("p (a k) -> p a k", k=P), qst[:, t % 2, h, :], kst[:, t - qt:t + 1, h, :],
                                                    start=False, stop=c == hb - 1, skip_group_check=True)
                    last.then_inc(s_full[i], 1)

            def stage_t(t):
                pe.wait_ge(s["m4"], t + 1)
                i = begin(t_full, t_free, tuse["M", t])
                nc.tensor.transpose(T[i][:, :].bitcast(bf16)[:, 0:P], mtok[:, t, :, :].rearrange("p g c -> p (g c)"),
                                    idb[:, :]).then_inc(t_full[i], 1)

            def stage_e(t, which):
                blks = blocks_of(t)
                for g in map(int, which):
                    pe.wait_ge(s["maug_ready"], NG * t + g + 1)
                    for k, (kt, diagonal) in enumerate(blks):
                        i = begin(s_full, s_free, suse["E", t, g, k])
                        for bank in range(2):
                            cols = SC[i][:, bank * D:(bank + 1) * D].rearrange("p (h q) -> p h q", q=P)
                            if diagonal:
                                nc.tensor.matmul(cols[:, :, :], idb[:, :],
                                                 mask_s[:, 1:2, :].broadcast_to([P, HG // 2, P]), start=True,
                                                 stop=False, skip_group_check=True)
                            for c in range(HG // 2):
                                h = g * HG + bank * (HG // 2) + c
                                last = nc.tensor.matmul(cols[:, c, :], kst[:, kt, h, :], qst[:, t % 2, h, :],
                                                        start=not diagonal, stop=(not diagonal) or c == HG // 2 - 1,
                                                        skip_group_check=True)
                        last.then_inc(s_full[i], 1)

            def stage_v(t, which):
                done(g_free, guse["A", t, 2])
                pe.wait_ge(s["const_ready"], 2)
                blks = blocks_of(t)
                for g in map(int, which):
                    if g % 2 == 0:
                        begin(t_full, t_free, tuse["E", t, g // 2])
                    i = tuse["E", t, g // 2][0]
                    for k in range(len(blks)):
                        done(s_free, suse["E", t, g, k])
                    for quad in range(2):
                        for k, (kt, _) in enumerate(blks):
                            for c in range(4):
                                col = (g % 2) * 2 + quad
                                last = nc.tensor.matmul(T[i][VW * c:VW * (c + 1), col * P:(col + 1) * P],
                                                        vaug[:, kt, g * HG + quad * 4 + c, :],
                                                        pt[:, nblk[t, g, k] % PTN, quad * 4 + c, :],
                                                        start=k == 0, stop=k == len(blks) - 1, skip_group_check=True)
                    last.then_inc(s["pv_done"] if g % 2 == 0 else t_full[i], 1)

            def stage_f(t, which):
                for half in map(int, which):
                    done(t_free, tuse["E", t, half])
                    i = begin(t_full, t_free, tuse["F", t, half])
                    for c in range(4):
                        last = nc.tensor.transpose(T[i][:, c * P:(c + 1) * P], osb[:, half, c * P:(c + 1) * P], idf[:, :])
                    last.then_inc(t_full[i], 1)

            def stage_p(t):
                for half in range(2):
                    done(t_free, tuse["F", t, half])
                i = begin(t_full, t_free, tuse["P", t])
                for c in range(KT):
                    last = nc.tensor.transpose(T[i][:, c * P:(c + 1) * P], att[:, c * P:(c + 1) * P], idf[:, :])
                last.then_inc(t_full[i], 1)

            def stage_o(t):
                if t == 0:
                    pe.wait_ge(ld["wo"], 16)
                done(t_free, tuse["P", t])
                i = begin(g_full, g_free, guse["O", t])
                project(G[i][:, :], attT, wo_s, KT).then_inc(g_full[i], 1)

            def stage_s(b):
                pe.wait_ge(s["q2_ready"], b + 1)
                pe.wait_ge(s["const_ready"], 2)
                i = begin(g_full, g_free, guse["S", b])
                for kt in range(CT):
                    last = nc.tensor.matmul(G[i][:, :], ones_b[:, :], q2_s[:, b, kt, :], start=kt == 0, stop=kt == CT - 1)
                last.then_inc(g_full[i], 1)

            def stage_g(t):
                pe.wait_ge(s["q1_ready"], t + 1)
                i = begin(t_full, t_free, tuse["G", t])
                for c in range(KT):
                    last = nc.tensor.transpose(T[i][:, :].bitcast(bf16)[:, c * P:(c + 1) * P], q1b[:, c * P:(c + 1) * P], idb[:, :])
                last.then_inc(t_full[i], 1)

            def stage_x(t):
                done(t_free, tuse["G", t])
                i = begin(g_full, g_free, guse["X", t])
                project(G[i][:, :], q1T, q2_s[:, t // QT, :, :], CT).then_inc(g_full[i], 1)

            def stage_h(t):
                pe.wait_ge(s["x2_ready"], t + 1)
                i = begin(t_full, t_free, tuse["H", t])
                for c in range(KT):
                    last = nc.tensor.transpose(T[i][:, c * P:(c + 1) * P], x2[:, t, c * P:(c + 1) * P], idf[:, :])
                last.then_inc(t_full[i], 1)

            def stage_r(t):
                if t == 0:
                    pe.wait_ge(ld["ar"], 16)
                done(t_free, tuse["H", t])
                i = begin(g_full, g_free, guse["R", t])
                project(G[i][:, 0:E + ER], x2T[:, t % 2, :, :], ar_s, KT).then_inc(g_full[i], 1)

            def stage_k(t):
                if t == 0:
                    pe.wait_ge(ld["wb"], 16)
                done(t_free, tuse["H", t])
                i = begin(g_full, g_free, guse["I", t])
                project(G[i][:, :], x2T[:, t % 2, :, :], wb_s, KT, stop=False)

            def stage_i(t):
                if t == 0:
                    pe.wait_ge(ld["lb"], 16)
                i = guse["I", t][0]
                pe.wait_ge(s["hw_ready"], t + 1)
                j = begin(t_full, t_free, tuse["I", t])
                nc.tensor.transpose(T[j][:, 0:P], hw[:, :, :].rearrange("p e r -> p (e r)"), idf[:, :]).then_inc(t_full[j], 1)
                done(t_free, tuse["I", t])
                nc.tensor.matmul(G[i][:, :], hwT[:, :], lb_s[:, :], start=False, stop=True).then_inc(g_full[i], 1)

            stages = {"A": stage_a, "B": stage_b, "C": stage_c, "T": stage_t, "E": stage_e, "V": stage_v,
                      "F": stage_f, "P": stage_p, "O": stage_o, "S": stage_s, "G": stage_g, "X": stage_x,
                      "H": stage_h, "R": stage_r, "K": stage_k, "I": stage_i}
            for st, t, which in ORDER:
                if st in stages:
                    stages[st](t, which) if which else stages[st](t)

        @block.vector
        def _(dve):
            def full(sems, use):
                dve.wait_ge(sems[use[0]], use[1])
                return use[0]

            def tile_stats(n, src):
                nc.vector.bn_stats(stl[:, n, :], src).then_inc(s["stl_ready"], 1)
                count["stl"] += 1
                dve.wait_ge(s["stl_ready"], count["stl"])
                nc.vector.bn_aggr(mvl[:, n, :], stl[:, n, :]).then_inc(s["mvl_ready"], 1)

            def normalise(n, t, dst, src, signal):
                dve.wait_ge(s["rsl_ready"], ln_number[n, t])
                nc.vector.tensor_scalar(dst, src, mvl[:, n, 0:1], rsl[:, n, 0:1], ALU.subtract, ALU.mult).then_inc(signal, 1)

            count = {"stl": 0}
            nc.vector.memset(ones_b[:, :], 1.0).then_inc(s["ones_ready"], 1)
            nc.vector.memset(halfs[:, :], -0.5).then_inc(s["const_ready"], 1)

            def stage_a(t, which):
                for j in ["kqv".index(c) for c in which]:
                    i = full(g_full, guse["A", t, j])
                    if j == 2:
                        nc.vector.tensor_scalar(vaug[:, t, :, 0:DH], G[i][:, :].rearrange("p (h d) -> p h d", d=DH),
                                                -CLIP, CLIP, ALU.max, ALU.min).then_inc(g_free[i], 1)
                        continue
                    if t >= 1:
                        dve.wait_ge(s["n1_ready"], 2 * (t - 1) + j + 1)
                    nc.vector.tensor_scalar(lin[:, j, :], G[i][:, :], -CLIP, CLIP, ALU.max, ALU.min).then_inc(g_free[i], 1)
                    dve.wait_ge(g_free[i], guse["A", t, j][1])
                    nc.vector.bn_stats(st6[:, j, :], lin[:, j, :]).then_inc(s["st_ready"], 1)
                    dve.wait_ge(s["st_ready"], 2 * t + j + 1)
                    if t >= 2:
                        dve.wait_ge(s["n2_ready"], 2 * (t - 2) + j + 1)
                    nc.vector.bn_aggr(mv[:, t % 2, j, :], st6[:, j, :]).then_inc(s["mv_ready"], 1)
                if t == 0 and "v" in which:
                    dve.wait_ge(ld["scal"], 16)
                    nc.vector.reciprocal(inv_s[:, :], scal_s[:, :].rearrange("p (a c) -> p a c", c=2)[:, :, 0]).then_inc(s["inv_ready"], 1)
                    nc.vector.memset(vaug[:, :, :, DH:VW], 0.0).then_inc(s["vones"], 1)
                    dve.wait_ge(s["vones"], 1)
                    nc.vector.memset(vaug[:, :, :, DH:DH + 1], 1.0).then_inc(s["const_ready"], 1)

            def stage_n(t, which):
                js = ["kq".index(c) for c in which]
                sl = t % 2
                for j in js:
                    if t >= 1:
                        dve.wait_ge(s["c3_ready"], 2 * (t - 1) + j + 1)
                    dve.wait_ge(s["mv_ready"], 2 * t + j + 1)
                    if t == 0:
                        if j == 0:
                            dve.wait_ge(ld_ln["k"], 16)
                        else:
                            dve.wait_ge(s["qln_scaled"], 1)
                    nc.vector.scalar_tensor_tensor(nrm[:, j, :], lin[:, j, :], mv[:, sl, j, 0:1], ln_s[:, 2 * j, :],
                                                   ALU.subtract, ALU.mult).then_inc(s["n1_ready"], 1)
                for j in js:
                    dve.wait_ge(s["n1_ready"], 2 * t + j + 1)
                    dve.wait_ge(s["rstd_ready"], 2 * t + j + 1)
                    nc.vector.scalar_tensor_tensor(nrm[:, j, :], nrm[:, j, :], rs2[:, sl, j:j + 1], ln_s[:, 2 * j + 1, :],
                                                   ALU.mult, ALU.add).then_inc(s["n2_ready"], 1)

            def stage_d(t, which):
                for j in ["kq".index(c) for c in which]:
                    at = FIRST[j][0] * DH
                    rest = nrm[:, j, :].rearrange("p (h d) -> p h d", d=DH)
                    dve.wait_ge(s["c1_ready"], 2 * t + j + 1)
                    nc.vector.tensor_tensor(rest, rest, stk[:, j, :, at:at + DH], ALU.subtract).then_inc(s["r_ready"], 1)

            def stage_w(t, which):
                if t >= 1:
                    return
                for j in ["kq".index(c) for c in which]:
                    second, third = SECOND[j][0] * DH, THIRD[j] * DH
                    rest = nrm[:, j, :].rearrange("p (h d) -> p h d", d=DH)
                    dve.wait_ge(s["c2_ready"], 2 * t + j + 1)
                    nc.vector.tensor_tensor(stk[:, j, :, third:third + DH], rest, stk[:, j, :, second:second + DH],
                                            ALU.subtract).then_inc(s["c3_ready"], 1)

            def stage_b(t, which):
                if t >= 2:
                    scores_done(dve, t - 2)
                for g in [2 * half + n for half in map(int, which) for n in range(2)]:
                    i = full(t_full, tuse["B", t, g])
                    nc.vector.tensor_copy(qst[0:PR, t % 2, g * HG:(g + 1) * HG, :],
                                          T[i][:, :].bitcast(bf16)[0:PR, :].rearrange("p (h q) -> p h q", q=P)).then_inc(t_free[i], 1)

            def stage_c(t, which):
                qt = t % QT
                per = HG // (1 + qt)
                for u in map(int, which):
                    i = full(s_full, suse["C", t, u])
                    nc.vector.tensor_reduce(mx[:, u * per:(u + 1) * per],
                                            SC[i][:, :].rearrange("p (h k) -> p h k", h=per), AX.X, ALU.max).then_inc(s_free[i], 1)

            def stage_m(t):
                for u in range(NG * (1 + t % QT)):
                    dve.wait_ge(s_free[suse["C", t, u][0]], suse["C", t, u][1])
                if t == 0:
                    dve.wait_ge(ld["mcols"], 16 * TILES)
                m_v = mx[:, :].rearrange("p (g c) -> p g c", c=HG)
                d_v = md[:, :].rearrange("p (g c) -> p g c", c=HG)
                nc.vector.tensor_scalar(mtok[:, t, :, 0:HG], m_v, -1.0, None, ALU.mult).then_inc(s["m1"], 1)
                dve.wait_ge(s["m1"], t + 1)
                nc.vector.scalar_tensor_tensor(d_v, m_v, -1.0, mtok[:, t, :, 0:HG], ALU.mult, ALU.subtract).then_inc(s["m2"], 1)
                dve.wait_ge(s["m2"], t + 1)
                nc.vector.tensor_copy(mtok[:, t, :, HG:2 * HG], d_v).then_inc(s["m3"], 1)
                dve.wait_ge(s["m3"], t + 1)
                nc.vector.tensor_tensor(mtok[:, t, :, 2 * HG:3 * HG], d_v, mtok[:, t, :, HG:2 * HG], ALU.subtract).then_inc(s["m4"], 1)

            def stage_u(t):
                i = full(t_full, tuse["M", t])
                nc.vector.tensor_copy(mT[:, :], T[i][:, :].bitcast(bf16)[:, 0:P]).then_inc(t_free[i], 1)
                dve.wait_ge(t_free[i], tuse["M", t][1])
                for g in range(NG):
                    nc.vector.tensor_copy(qst[P - AUG:P, t % 2, g * HG:(g + 1) * HG, :],
                                          mT[AUG * g:AUG * (g + 1), :].unsqueeze(1).broadcast_to([AUG, HG, P])
                                          ).then_inc(s["maug_ready"], 1)

            def stage_f(t, which):
                for half in map(int, which):
                    i = full(t_full, tuse["F", t, half])
                    o = T[i][:, :].rearrange("p (h c) -> p h c", c=VW)
                    nc.vector.reciprocal(rsum[:, half, :], o[:, :, DH]).then_inc(s["rsum_ready"], 1)
                    dve.wait_ge(s["rsum_ready"], 2 * t + half + 1)
                    if t >= 1:
                        dve.wait_ge(t_full[tuse["P", t - 1][0]], tuse["P", t - 1][1])
                    nc.vector.tensor_tensor(att[:, half * 256:(half + 1) * 256].rearrange("p (h d) -> p h d", d=DH),
                                            o[:, :, 0:DH], rsum[:, half, :].unsqueeze(2).broadcast_to([P, H // 2, DH]),
                                            ALU.mult).then_inc(t_free[i], 1)

            def stage_o(t):
                i = full(g_full, guse["O", t])
                if t == 0:
                    dve.wait_ge(ld["xrow"], 16)
                if t >= 1:
                    dve.wait_ge(s["q1_ready"], t)
                nc.vector.tensor_tensor(r1[:, :], G[i][:, :], x_s[:, t, :], ALU.add).then_inc(g_free[i], 1)
                dve.wait_ge(g_free[i], guse["O", t][1])
                tile_stats(0, r1[:, :])

            def stage_q(t):
                normalise(0, t, x1[:, t, :], r1[:, :], s["x1_ready"])
                dve.wait_ge(s["x1_ready"], t + 1)
                nc.vector.tensor_scalar(qd[:, :], x1[:, t, :], inv_s[:, 0:1], scal_s[:, 1:2], ALU.mult, ALU.add).then_inc(s["qd1"], 1)
                dve.wait_ge(s["qd1"], t + 1)
                nc.vector.tensor_scalar(qd[:, :], qd[:, :], QMAX, ROUND, ALU.min, ALU.add).then_inc(s["qd2"], 1)
                dve.wait_ge(s["qd2"], t + 1)
                if t >= 1:
                    dve.wait_ge(s["rowsum_ready"], t)
                    full(t_full, tuse["G", t - 1])
                nc.vector.tensor_scalar(q1b[:, :], qd[:, :], ROUND, -(ROUND + CENTRE), ALU.max, ALU.add).then_inc(s["q1_ready"], 1)

            def stage_s(b):
                if b == 0:
                    z = scal_s[:, :].rearrange("p (a c) -> p a c", c=2)
                    nc.vector.tensor_scalar(a12[:, :], z[:, :, 1], -1.0, CENTRE, ALU.mult, ALU.add).then_inc(s["sc1"], 1)
                    nc.vector.tensor_tensor(s12[:, :], scal_s[:, 0:1], scal_s[:, 2:3], ALU.mult).then_inc(s["sc1"], 1)
                    dve.wait_ge(s["sc1"], 2)
                    nc.vector.tensor_scalar(kaa[:, :], a12[:, 0:1], a12[:, 1:2], float(CTX), ALU.mult, ALU.mult).then_inc(s["sc2"], 1)
                    dve.wait_ge(s["sc2"], 1)
                i = full(g_full, guse["S", b])
                nc.vector.tensor_scalar(colc[:, b, :], G[i][:, :], a12[:, 0:1], kaa[:, :], ALU.mult, ALU.add).then_inc(g_free[i], 1)

            def stage_z(b):
                dve.wait_ge(s["q2a"], b + 1)
                nc.vector.tensor_scalar(ctx_s[:, :, :], ctx_s[:, :, :], QMAX, ROUND, ALU.min, ALU.add).then_inc(s["q2b"], 1)
                dve.wait_ge(s["q2b"], b + 1)
                nc.vector.tensor_scalar(q2_s[:, b, :, :], ctx_s[:, :, :], ROUND, -(ROUND + CENTRE), ALU.max,
                                        ALU.add).then_inc(s["q2_ready"], 1)

            def stage_x(t):
                b = t // QT
                dve.wait_ge(s["rowsum_ready"], t + 1)
                nc.vector.tensor_tensor(arq[:, :], rsq[:, :], a12[:, 1:2], ALU.mult).then_inc(s["arq_ready"], 1)
                dve.wait_ge(s["arq_ready"], t + 1)
                i = full(g_full, guse["X", t])
                dve.wait_ge(g_free[guse["S", b][0]], guse["S", b][1])
                if t >= 1:
                    dve.wait_ge(s["x2_ready"], t)
                nc.vector.scalar_tensor_tensor(r2[:, :], G[i][:, :], arq[:, :], colc[:, b, :], ALU.add, ALU.add).then_inc(g_free[i], 1)
                dve.wait_ge(g_free[i], guse["X", t][1])
                nc.vector.scalar_tensor_tensor(r2[:, :], r2[:, :], s12[:, :], x1[:, t, :], ALU.mult, ALU.add).then_inc(s["r2_ready"], 1)
                dve.wait_ge(s["r2_ready"], t + 1)
                tile_stats(1, r2[:, :])

            def stage_y(t):
                normalise(1, t, x2[:, t, :], r2[:, :], s["x2_ready"])

            def stage_r(t):
                i = full(g_full, guse["R", t])
                sl = t % 2
                nc.vector.tensor_copy(lg[:, sl, :], G[i][:, 0:E + ER]).then_inc(g_free[i], 1)
                dve.wait_ge(g_free[i], guse["R", t][1])
                nc.vector.max(top[:, :], lg[:, sl, 0:E]).then_inc(s["top_ready"], 1)
                dve.wait_ge(s["top_ready"], t + 1)
                if t >= 1:
                    dve.wait_ge(s["ex_ready"], t)
                nc.vector.tensor_tensor(dl[:, :], top[:, 1:2], top[:, 0:1], ALU.subtract).then_inc(s["dl_ready"], 1)
                nc.vector.max_index(idx[:, :], top[:, :], lg[:, sl, 0:E]).then_inc(s["idx_ready"], 1)
                dve.wait_ge(s["idx_ready"], t + 1)
                nc.vector.tensor_copy(idxf[:, :], idx[:, 0:2]).then_inc(s["idxf_ready"], 1)

            def stage_weigh(t):
                sl = t % 2
                dve.wait_ge(s["ex_ready"], t + 1)
                nc.vector.tensor_scalar(den[:, :], ex[:, :], 1.0, 1.0 / LORA_SCALE, ALU.add, ALU.mult).then_inc(s["den_ready"], 1)
                dve.wait_ge(s["den_ready"], t + 1)
                nc.vector.reciprocal(w01[:, 0:1], den[:, :]).then_inc(s["w0_ready"], 1)
                dve.wait_ge(s["w0_ready"], t + 1)
                nc.vector.tensor_tensor(w01[:, 1:2], w01[:, 0:1], ex[:, :], ALU.mult).then_inc(s["w1_ready"], 1)
                dve.wait_ge(s["w1_ready"], t + 1)
                dve.wait_ge(s["idxf_ready"], t + 1)
                for j in range(2):
                    nc.vector.tensor_scalar(wsel[:, j, :], iota_s[:, :], idxf[:, j:j + 1], w01[:, j:j + 1],
                                            ALU.is_equal, ALU.mult).then_inc(s["ws0"], 1)
                dve.wait_ge(s["ws0"], 2 * t + 2)
                nc.vector.tensor_tensor(wsel[:, 0, :], wsel[:, 0, :], wsel[:, 1, :], ALU.add).then_inc(s["wsel_ready"], 1)
                dve.wait_ge(s["wsel_ready"], t + 1)
                if t >= 1:
                    dve.wait_ge(t_full[tuse["I", t - 1][0]], tuse["I", t - 1][1])
                nc.vector.tensor_tensor(hw[:, :, :], lg[:, sl, E:E + ER].rearrange("p (e r) -> p e r", r=R),
                                        wsel[:, 0, :].unsqueeze(2).broadcast_to([P, E, R]), ALU.mult).then_inc(s["hw_ready"], 1)

            def stage_i(t):
                i = full(g_full, guse["I", t])
                dve.wait_ge(s["xb_ready"], t + 1)
                if t >= 1:
                    dve.wait_ge(s["x3_ready"], t)
                nc.vector.tensor_tensor(r3[:, :], G[i][:, :], xb[:, t % 2, :], ALU.add).then_inc(g_free[i], 1)
                dve.wait_ge(g_free[i], guse["I", t][1])
                tile_stats(2, r3[:, :])

            def stage_j(t):
                normalise(2, t, x3[:, t, :], r3[:, :], s["x3_ready"])

            stages = {"A": stage_a, "N": stage_n, "B": stage_b, "C": stage_c, "M": stage_m, "U": stage_u,
                      "D": stage_d, "W": stage_w, "F": stage_f, "O": stage_o, "S": stage_s, "X": stage_x,
                      "R": stage_r, "w": stage_weigh, "I": stage_i, "Z": stage_z, "Q": stage_q, "Y": stage_y,
                      "J": stage_j}
            for st, t, which in ORDER:
                if st in stages:
                    stages[st](t, which) if which else stages[st](t)

        @block.scalar
        def _(act):
            def values_done(m):
                t, g = m
                if g % 2 == 0:
                    act.wait_ge(s["pv_done"], NG // 2 * t + g // 2 + 1)
                else:
                    full(t_full, tuse["E", t, g // 2])

            def full(sems, use):
                act.wait_ge(sems[use[0]], use[1])
                return use[0]

            def stage_l(_):
                act.wait_ge(ld_ln["q"], 16)
                nc.scalar.activation(ln_s[:, 2:4, :], ln_s[:, 2:4, :], ACT.Copy, scale=DH ** -0.5).then_inc(s["qln_scaled"], 1)

            def stage_z(b):
                act.wait_ge(ld["ctx"], 16 * (b + 1))
                act.wait_ge(s["inv_ready"], 1)
                nc.scalar.activation(ctx_s[:, :, :], ctx_s[:, :, :], ACT.Identity, bias=scal_s[:, 3:4],
                                     scale=inv_s[:, 1:2]).then_inc(s["q2a"], 1)

            def stage_n(t, which):
                js = ["kq".index(c) for c in which]
                for j in js:
                    act.wait_ge(s["n2_ready"], 2 * t + j + 1)
                    if t >= 1:
                        for n in range(2):
                            if j == 0:
                                full(s_full, suse["B", t - 1, n])
                            else:
                                full(t_full, tuse["B", t - 1, NG - 1 - n])
                    at = FIRST[j][0]
                    nc.scalar.activation(
                        stk[:, j, :, at * DH:(at + 3) * DH].rearrange("p h (a d) -> p h a d", d=DH),
                        nrm[:, j, :].rearrange("p (h d) -> p h d", d=DH).unsqueeze(2).broadcast_to([P, H, 3, DH]),
                        ACT.Copy).then_inc(s["c1_ready"], 1)

            def stage_d(t, which):
                for j in ["kq".index(c) for c in which]:
                    act.wait_ge(s["r_ready"], 2 * t + j + 1)
                    at, last = SECOND[j]
                    step = last - at
                    parts = stk[:, j, :, :].rearrange("p h (a d) -> p h a d", d=DH)
                    nc.scalar.activation(
                        parts[:, :, at:last + 1:step, :],
                        nrm[:, j, :].rearrange("p (h d) -> p h d", d=DH).unsqueeze(2).broadcast_to([P, H, 2, DH]),
                        ACT.Copy).then_inc(s["c2_ready"], 1)

            def stage_b(t, which):
                for half in map(int, which):
                    i = full(s_full, suse["B", t, half])
                    nc.scalar.activation(kst[0:PR, t, half * (H // 2):(half + 1) * (H // 2), :],
                                         SC[i][:, :].bitcast(bf16)[0:PR, :].rearrange("p (h q) -> p h q", q=P),
                                         ACT.Copy).then_inc(s_free[i], 1)

            def stage_e(t, which):
                for g in map(int, which):
                    for k in range(len(blocks_of(t))):
                        i = full(s_full, suse["E", t, g, k])
                        n = nblk[t, g, k]
                        if n >= PTN:
                            values_done(grp_of[n - PTN])
                        nc.scalar.activation(pt[:, n % PTN, :, :].rearrange("p h q -> p (h q)"), SC[i][:, :], ACT.Exp).then_inc(s_free[i], 1)

            def stage_v(t, which):
                for half in [g // 2 for g in map(int, which) if g % 2 == 1]:
                    i = full(t_full, tuse["E", t, half])
                    if t >= 1:
                        act.wait_ge(t_full[tuse["F", t - 1, half][0]], tuse["F", t - 1, half][1])
                    nc.scalar.activation(osb[:, half, :], T[i][:, :], ACT.Copy).then_inc(t_free[i], 1)

            def stage_p(t):
                i = full(t_full, tuse["P", t])
                if t >= 1:
                    full(g_full, guse["O", t - 1])
                nc.scalar.activation(attT[:, :, :].rearrange("p a b -> p (a b)"), T[i][:, :], ACT.Copy).then_inc(t_free[i], 1)

            def stage_g(t):
                i = full(t_full, tuse["G", t])
                if t >= 1:
                    full(g_full, guse["X", t - 1])
                nc.scalar.activation(q1T[:, :, :].rearrange("p a b -> p (a b)"), T[i][:, :].bitcast(bf16)[:, 0:D], ACT.Copy).then_inc(t_free[i], 1)
                if t >= 1:
                    act.wait_ge(s["arq_ready"], t)
                nc.scalar.activation(unread[:, :], q1b[:, :], ACT.Copy, accum_out=rsq[:, :]).then_inc(s["rowsum_ready"], 1)

            def stage_h(t):
                i = full(t_full, tuse["H", t])
                nc.scalar.activation(x2T[:, t % 2, :, :].rearrange("p a b -> p (a b)"), T[i][:, :], ACT.Copy).then_inc(t_free[i], 1)

            def stage_r(t):
                act.wait_ge(s["dl_ready"], t + 1)
                if t >= 1:
                    act.wait_ge(s["w1_ready"], t)
                nc.scalar.activation(ex[:, :], dl[:, :], ACT.Exp).then_inc(s["ex_ready"], 1)

            def stage_i(t):
                i = full(t_full, tuse["I", t])
                if t >= 1:
                    full(g_full, guse["I", t - 1])
                nc.scalar.activation(hwT[:, :], T[i][:, 0:P], ACT.Copy).then_inc(t_free[i], 1)

            stages = {"L": stage_l, "N": stage_n, "D": stage_d, "B": stage_b, "E": stage_e, "V": stage_v,
                      "P": stage_p, "G": stage_g, "H": stage_h, "R": stage_r, "I": stage_i, "Z": stage_z}
            for st, t, which in ORDER:
                if st in stages:
                    stages[st](t, which) if which else stages[st](t)

        @block.gpsimd
        def _(pool):
            def rstd(dst, tmp, var, n, ready, mid):
                nc.gpsimd.tensor_scalar(tmp, var, EPS, None, ALU.add).then_inc(s[mid], 1)
                count[mid] += 1
                pool.wait_ge(s[mid], count[mid])
                nc.gpsimd.tensor_tensor(dst, tmp, halfs[:, 0:n], ALU.pow).then_inc(s[ready], 1)
                count[ready] += 1

            count = {"ve_ready": 0, "rstd_ready": 0, "vel_ready": 0, "rsl_ready": 0}

            def stage_a(t, which):
                sl = t % 2
                if t == 0 and "k" in which:
                    pool.wait_ge(s["const_ready"], 1)
                for j in ["kqv".index(c) for c in which if c != "v"]:
                    pool.wait_ge(s["mv_ready"], 2 * t + j + 1)
                    rstd(rs2[:, sl, j:j + 1], ve2[:, j:j + 1], mv[:, sl, j, 1:2], 1, "rstd_ready", "ve_ready")

            def stage_o(t):
                ln_rstd(0)

            def stage_w(t, which):
                for j in ["kq".index(c) for c in which]:
                    if t == 0:
                        continue
                    second, third = SECOND[j][0] * DH, THIRD[j] * DH
                    rest = nrm[:, j, :].rearrange("p (h d) -> p h d", d=DH)
                    pool.wait_ge(s["c2_ready"], 2 * t + j + 1)
                    nc.gpsimd.tensor_tensor(stk[:, j, :, third:third + DH], rest, stk[:, j, :, second:second + DH],
                                            ALU.subtract).then_inc(s["c3_ready"], 1)

            def ln_rstd(n):
                count["mvl"] = count.get("mvl", 0) + 1
                pool.wait_ge(s["mvl_ready"], count["mvl"])
                rstd(rsl[:, n, :], vel[:, n, :], mvl[:, n, 1:2], 1, "rsl_ready", "vel_ready")

            def stage_x(t):
                ln_rstd(1)

            def stage_y(t):
                pool.wait_ge(s["x2_ready"], t + 1)
                if t == 0:
                    pool.wait_ge(ld_ln["base"], 16)
                if t >= 2:
                    pool.wait_ge(g_free[guse["I", t - 2][0]], guse["I", t - 2][1])
                nc.gpsimd.tensor_tensor(xb[:, t % 2, :], x2[:, t, :], ln_s[:, 4, :], ALU.add).then_inc(s["xb_ready"], 1)
                count["xb_ready"] = t + 1

            def stage_i(t):
                ln_rstd(2)

            stages = {"A": stage_a, "W": stage_w, "O": stage_o, "X": stage_x, "Y": stage_y, "I": stage_i}
            for st, t, which in ORDER:
                if st in stages:
                    stages[st](t, which) if which else stages[st](t)


def three_parts(a):
    bfloat16 = mybir.dt.np(mybir.dt.bfloat16)
    a = a.astype(np.float64)
    hi = a.astype(np.float32).astype(bfloat16)
    mid = (a - hi.astype(np.float64)).astype(np.float32).astype(bfloat16)
    lo = (a - hi.astype(np.float64) - mid.astype(np.float64)).astype(np.float32).astype(bfloat16)
    return hi, mid, lo


def constants():
    bfloat16 = mybir.dt.np(mybir.dt.bfloat16)
    ident = np.eye(P, dtype=np.float32)
    i = np.arange(P)
    mask = np.where(i[:, None] >= i[None, :], 0.0, MASKED).astype(np.float32)
    masks = np.stack([mask, mask.T], axis=1).astype(bfloat16)
    slopes = (1.0 / np.power(np.float32(2.0), np.arange(1, H + 1, dtype=np.float32) * np.float32(8.0 / H))).astype(np.float32)
    pos = np.arange(S)
    kaug = np.zeros((AUG, QT, H, P), dtype=bfloat16)
    rise = three_parts(slopes[:, None].astype(np.float64) * pos[None, :])
    fall = three_parts(-slopes)
    for h in range(H):
        for part in range(3):
            kaug[part * HG + h % HG, :, h, :] = 1.0
            kaug[3 * HG + part, :, h, :] = rise[part][h].reshape(QT, P)
            kaug[3 * HG + 3 + part, :, h, :] = fall[part][h]
    qaug = np.zeros((AUG, QT, P), dtype=bfloat16)
    qaug[3 * HG:3 * HG + 3] = 1.0
    qaug[3 * HG + 3:3 * HG + 6] = pos.reshape(QT, P)[None]
    mcols = np.zeros((QT, P, H // HG, AUG), dtype=bfloat16)
    mcols[:] = np.transpose(qaug, (1, 2, 0))[:, :, None, :]
    iota = np.broadcast_to(np.arange(E, dtype=np.float32), (P, E)).copy()
    qaug = np.ascontiguousarray(np.broadcast_to(qaug.transpose(1, 0, 2)[:, :, None, :], (QT, AUG, H, P)))
    return ident, ident.astype(bfloat16), masks, kaug, qaug, mcols, iota


def kernel(**inputs):
    import concourse.bacc as _bacc
    from concourse.bass_utils import run_bass_kernel_spmd as _run

    f = {k: np.asarray(v) for k, v in inputs.items()}

    def rows(w, n):
        return np.ascontiguousarray(w.reshape(-1, P, n).transpose(1, 0, 2))

    x = f["x"].reshape(B * S, D)
    xT = np.ascontiguousarray(x.reshape(TILES, P, KT, P).transpose(0, 3, 2, 1))
    xrow = np.ascontiguousarray(x.reshape(TILES, P, D).transpose(1, 0, 2))
    wq, wk, wv = f["L0_attn_w_qkv"].reshape(3, D, D)
    wqkvT = np.stack([rows(w.T, D) for w in (wk, wq, wv)])
    ln = np.stack([f["L0_attn_k_ln_w"], f["L0_attn_k_ln_b"], f["L0_attn_q_ln_w"], f["L0_attn_q_ln_b"], f["L0_ffn_b_base"]])
    ln = ln[None]
    woT = rows(f["L0_attn_w_out"].T, D)
    ctx4 = np.stack([rows(f["ctx_4096"][b], D) for b in range(B)])
    scal = np.concatenate([f["L0_xattn_x1_scale"], f["L0_xattn_x1_zp"], f["L0_xattn_x2_scale"], f["L0_xattn_x2_zp"]])
    scal = np.ascontiguousarray(np.broadcast_to(scal, (P, 4)))
    wbT = rows(f["L0_ffn_W_base"].T, D)
    arT = rows(np.concatenate([f["L0_ffn_W_router"], f["L0_ffn_A"].reshape(ER, D)]).T, E + ER)
    loraB = np.ascontiguousarray(f["L0_ffn_B"].transpose(0, 2, 1).reshape(ER, D))
    ident, identb, masks, kaug, qaug, mcols, iota = constants()

    nc = _bacc.Bacc("TRN2", target_bir_lowering=False, num_devices=1)
    arrays, args = {}, []
    for name, a in dict(xT=xT, xrow=xrow, wqkvT=wqkvT, ln=ln, woT=woT, ctx4=ctx4, scal=scal, wbT=wbT, arT=arT, loraB=loraB,
                        identf=ident, identb=identb, maskc=masks, kaug=kaug, qaug=qaug, mcols=mcols, iota=iota).items():
        a = np.ascontiguousarray(a)
        arrays[name + "_dram"] = a
        args.append(nc.dram_tensor(name + "_dram", a.shape, mybir.dt.from_np(a.dtype), kind="ExternalInput").ap())
    out = nc.dram_tensor("out_dram", (TILES, P, D), mybir.dt.float32, kind="ExternalOutput").ap()
    build(nc, *args, out)
    r = _run(nc, [arrays], core_ids=[0])
    return r.results[0]["out_dram"].reshape(B, S, D)
```
